# Optimizing a Trainium2 kernel written in Bass

```python
import numpy as np
import jax
import jax.numpy as jnp

def _softmax(x, axis=-1):
    return jax.nn.softmax(x, axis=axis)

def _gelu(x):
    return jax.nn.gelu(x, approximate=True)

def _silu(x):
    return jax.nn.silu(x)

def _sigmoid(x):
    return jax.nn.sigmoid(x)

def _layernorm(x, axis=-1, eps=1e-05):
    m = jnp.mean(x, axis=axis, keepdims=True)
    v = jnp.var(x, axis=axis, keepdims=True)
    return (x - m) / jnp.sqrt(v + eps)

def _scatter_add(tgt, idx, src, axis=0):
    return tgt.at[idx].add(src)

def _segment_sum(src, seg, n):
    return jax.ops.segment_sum(src, seg, n)
kernel_name = 'mk_flamingo_gated_d2_seqx_r8_9ca47d'

def setup_inputs(seed: int=0):
    np.random.seed(seed)
    _w = jnp.asarray

    def _rec_inputs():
        import jax
        import jax.numpy as jnp
        _rk = jax.random.key(seed)
        x = 7.22e-05 + 1 * jax.random.normal(jax.random.fold_in(_rk, 1), (16, 256, 128), jnp.float32)
        _lenS = 256 - jax.random.randint(jax.random.fold_in(_rk, 7), (16,), 0, max(1, 256 // 4) + 1, jnp.int32)
        _lenS2 = 1601 - jax.random.randint(jax.random.fold_in(_rk, 8), (16,), 0, max(1, 1601 // 4) + 1, jnp.int32)
        _ctx_768P = jax.random.normal(jax.random.fold_in(_rk, 11), (16, 16, 96), jnp.float32)
        _ctx_768c = jax.random.dirichlet(jax.random.fold_in(_rk, 511), 0.3 * jnp.ones((16,), jnp.float32), (16, 1601))
        _ctx_768t = jnp.einsum('bsk,bkd->bsd', _ctx_768c, _ctx_768P)
        _ctx_768t = _ctx_768t * jax.lax.rsqrt(jnp.mean(jnp.square(_ctx_768t)) + 1e-12) * 0.953939
        ctx_768 = 3.88148e-05 + 0.999967 * (_ctx_768t + 0.3 * jax.random.normal(jax.random.fold_in(_rk, 611), (16, 1601, 96), jnp.float32))
        _validS = jnp.arange(256)[None, :] < _lenS[:, None]
        _validS2 = jnp.arange(1601)[None, :] < _lenS2[:, None]
        _causal = jnp.tril(jnp.ones((256, 256), dtype=bool))
        mask_BxS_bf1 = jnp.ones((16, 256), dtype=bool)
        mask_BxS2_bf1 = jnp.ones((16, 1601), dtype=bool)
        _g = jax.random.normal(jax.random.fold_in(_rk, 9001), (2, 2), jnp.float32)
        _g = jnp.sign(_g) * jnp.maximum(jnp.abs(_g), 1.0) + (_g == 0) * 1.0
        g_xattn = _g[0]
        g_ffn = _g[1]
        return (x, ctx_768, mask_BxS_bf1, mask_BxS2_bf1, g_xattn, g_ffn)
    x, ctx_768, mask_BxS_bf1, mask_BxS2_bf1, g_xattn, g_ffn = _rec_inputs()

    def _L0_xattn_setup():
        import jax, jax.numpy as jnp
        import numpy as np
        B, T, DT, G, DV = (16, 64, 128, 72, 96)
        H, DH = (4, 32)
        INNER = H * DH
        HID = 4 * DT
        N_STATE = 64
        K_TOP = 32

        def layernorm(x, g, b, eps=1e-05):
            m = x.mean(-1, keepdims=True)
            v = x.var(-1, keepdims=True)
            return (x - m) * jax.lax.rsqrt(v + eps) * g + b

        def s4d(x, log_dt, A_re, A_im, C_re, C_im, D_skip):
            Bb, L, D = x.shape
            dt = jnp.exp(log_dt)
            A = A_re + 1j * A_im
            C = C_re + 1j * C_im
            dtA = dt[:, None] * A
            dC = C * (jnp.exp(dtA) - 1.0) / A
            powers = jnp.exp(dtA[:, :, None] * jnp.arange(L))
            K = 2.0 * jnp.einsum('dn,dnl->dl', dC, powers).real
            n = 2 * L
            Kf = jnp.fft.rfft(K, n=n, axis=-1)
            xf = jnp.fft.rfft(x, n=n, axis=1)
            y = jnp.fft.irfft(xf * Kf.T[None], n=n, axis=1)[:, :L]
            return y + x * D_skip
        key = jax.random.key(seed)
        ks = jax.random.split(key, 16)
        s = 0.02
        inp = {'x_text': jax.random.normal(ks[0], (B, T, DT), jnp.float32), 'x_vision': jax.random.normal(ks[1], (B, G, DV), jnp.float32), 'text_mask': jnp.ones((B, T), bool), 'vision_mask': jnp.ones((B, G), bool), 'Wq': jax.random.normal(ks[2], (DT, INNER), jnp.float32) * s, 'Wk': jax.random.normal(ks[3], (DV, INNER), jnp.float32) * s, 'Wv': jax.random.normal(ks[4], (DV, DT), jnp.float32) * s, 'W_film_in': jax.random.normal(ks[5], (DT, 2 * DT), jnp.float32) * s, 'b_film_in': jnp.zeros((2 * DT,), jnp.float32), 'W_film_out': jax.random.normal(ks[6], (DT, 2 * DT), jnp.float32) * s, 'b_film_out': jnp.zeros((2 * DT,), jnp.float32), 'g_norm_in': jnp.ones((DT,), jnp.float32), 'b_norm_in': jnp.zeros((DT,), jnp.float32), 'g_norm_out': jnp.ones((DT,), jnp.float32), 'b_norm_out': jnp.zeros((DT,), jnp.float32), 'g_ffn': jnp.ones((DT,), jnp.float32), 'b_ffn': jnp.zeros((DT,), jnp.float32), 'W1': jax.random.normal(ks[7], (DT, HID), jnp.float32) * s, 'b1': jnp.zeros((HID,), jnp.float32), 'W2': jax.random.normal(ks[8], (HID, DT), jnp.float32) * s, 'b2': jnp.zeros((DT,), jnp.float32), 'log_dt': jnp.log(0.001) + jax.random.uniform(ks[9], (DT,), jnp.float32) * (jnp.log(0.1) - jnp.log(0.001)), 'A_re': -0.5 * jnp.ones((DT, N_STATE), jnp.float32), 'A_im': jnp.tile(jnp.pi * jnp.arange(N_STATE, dtype=jnp.float32), (DT, 1)), 'C_re': jax.random.normal(ks[10], (DT, N_STATE), jnp.float32) * 0.5 ** 0.5, 'C_im': jax.random.normal(ks[11], (DT, N_STATE), jnp.float32) * 0.5 ** 0.5, 'D_skip': jax.random.normal(ks[12], (DT,), jnp.float32), 'mod_gate': jnp.array(0.5, jnp.float32)}
        return inp
    _L0_xattn_all = _L0_xattn_setup()
    _L0_xattn_in = {k: v for k, v in _L0_xattn_all.items() if k in ('Wq', 'Wk', 'Wv', 'W_film_in', 'b_film_in', 'W_film_out', 'b_film_out', 'g_norm_in', 'b_norm_in', 'g_norm_out', 'b_norm_out', 'g_ffn', 'b_ffn', 'W1', 'b1', 'W2', 'b2', 'log_dt', 'A_re', 'A_im', 'C_re', 'C_im', 'D_skip', 'mod_gate')}
    del _L0_xattn_all

    def _L0_ffn_setup():
        import jax, jax.numpy as jnp
        import numpy as np
        H = 128
        E = 8
        B, S = (4, 256)
        key = jax.random.key(seed)
        k1, k2, k3, k4 = jax.random.split(key, 4)
        x = jax.random.normal(k1, (B, S, H), dtype=jnp.float32)
        wg = jax.random.normal(k2, (H, E), dtype=jnp.float32) * 0.02
        W = jax.random.normal(k3, (E, H, H), dtype=jnp.float32) * 0.02
        b = jax.random.normal(k4, (E, H), dtype=jnp.float32) * 0.02
        return {'x': x, 'wg': wg, 'W': W, 'b': b}
    _L0_ffn_all = _L0_ffn_setup()
    _L0_ffn_in = {k: v for k, v in _L0_ffn_all.items() if k in ('wg', 'W', 'b')}
    del _L0_ffn_all

    def _L1_xattn_setup():
        import jax, jax.numpy as jnp
        import numpy as np
        N_HEADS = 16
        DIMS = 128
        D_CTX = 96
        HEAD = DIMS // N_HEADS
        key = jax.random.key(seed)
        ks = jax.random.split(key, 10)
        s_q = 1.0 / np.sqrt(DIMS)
        s_c = 1.0 / np.sqrt(D_CTX)
        return {'x': jax.random.normal(ks[0], (2, 256, DIMS), jnp.float32), 'context': jax.random.normal(ks[1], (2, 256, D_CTX), jnp.float32), 'w_q': jax.random.normal(ks[2], (DIMS, DIMS), jnp.float32) * s_q, 'b_q': jax.random.normal(ks[3], (DIMS,), jnp.float32) * 0.01, 'w_k': jax.random.normal(ks[4], (D_CTX, DIMS), jnp.float32) * s_c, 'b_k': jax.random.normal(ks[5], (DIMS,), jnp.float32) * 0.01, 'w_v': jax.random.normal(ks[6], (D_CTX, DIMS), jnp.float32) * s_c, 'b_v': jax.random.normal(ks[7], (DIMS,), jnp.float32) * 0.01, 'w_o': jax.random.normal(ks[8], (DIMS, DIMS), jnp.float32) * s_q, 'b_o': jax.random.normal(ks[9], (DIMS,), jnp.float32) * 0.01}
    _L1_xattn_all = _L1_xattn_setup()
    _L1_xattn_in = {k: v for k, v in _L1_xattn_all.items() if k in ('w_q', 'b_q', 'w_k', 'b_k', 'w_v', 'b_v', 'w_o', 'b_o')}
    del _L1_xattn_all

    def _L1_ffn_setup():
        import jax, jax.numpy as jnp
        import numpy as np
        B, T, D, H, E = (4, 256, 128, 512, 8)
        key = jax.random.key(seed)
        ks = jax.random.split(key, 7)
        x = jax.random.normal(ks[0], (B, T, D), dtype=jnp.float32)
        Wg = jax.random.normal(ks[1], (D, E), dtype=jnp.float32) / np.sqrt(D)
        bg = jax.random.normal(ks[2], (E,), dtype=jnp.float32) * 0.01
        W1 = jax.random.normal(ks[3], (E, D, H), dtype=jnp.float32) / np.sqrt(D)
        b1 = jax.random.normal(ks[4], (E, H), dtype=jnp.float32) * 0.01
        W2 = jax.random.normal(ks[5], (E, H, D), dtype=jnp.float32) / np.sqrt(H)
        b2 = jax.random.normal(ks[6], (E, D), dtype=jnp.float32) * 0.01
        return {'x': x, 'Wg': Wg, 'bg': bg, 'W1': W1, 'b1': b1, 'W2': W2, 'b2': b2}
    _L1_ffn_all = _L1_ffn_setup()
    _L1_ffn_in = {k: v for k, v in _L1_ffn_all.items() if k in ('Wg', 'bg', 'W1', 'b1', 'W2', 'b2')}
    del _L1_ffn_all
    return {'x': x, 'ctx_768': ctx_768, 'mask_BxS_bf1': mask_BxS_bf1, 'mask_BxS2_bf1': mask_BxS2_bf1, 'g_xattn': g_xattn, 'g_ffn': g_ffn, 'L0_xattn_Wq': _L0_xattn_in['Wq'], 'L0_xattn_Wk': _L0_xattn_in['Wk'], 'L0_xattn_Wv': _L0_xattn_in['Wv'], 'L0_xattn_W_film_in': _L0_xattn_in['W_film_in'], 'L0_xattn_b_film_in': _L0_xattn_in['b_film_in'], 'L0_xattn_W_film_out': _L0_xattn_in['W_film_out'], 'L0_xattn_b_film_out': _L0_xattn_in['b_film_out'], 'L0_xattn_g_norm_in': _L0_xattn_in['g_norm_in'], 'L0_xattn_b_norm_in': _L0_xattn_in['b_norm_in'], 'L0_xattn_g_norm_out': _L0_xattn_in['g_norm_out'], 'L0_xattn_b_norm_out': _L0_xattn_in['b_norm_out'], 'L0_xattn_g_ffn': _L0_xattn_in['g_ffn'], 'L0_xattn_b_ffn': _L0_xattn_in['b_ffn'], 'L0_xattn_W1': _L0_xattn_in['W1'], 'L0_xattn_b1': _L0_xattn_in['b1'], 'L0_xattn_W2': _L0_xattn_in['W2'], 'L0_xattn_b2': _L0_xattn_in['b2'], 'L0_xattn_log_dt': _L0_xattn_in['log_dt'], 'L0_xattn_A_re': _L0_xattn_in['A_re'], 'L0_xattn_A_im': _L0_xattn_in['A_im'], 'L0_xattn_C_re': _L0_xattn_in['C_re'], 'L0_xattn_C_im': _L0_xattn_in['C_im'], 'L0_xattn_D_skip': _L0_xattn_in['D_skip'], 'L0_xattn_mod_gate': _L0_xattn_in['mod_gate'], 'L0_ffn_wg': _L0_ffn_in['wg'], 'L0_ffn_W': _L0_ffn_in['W'], 'L0_ffn_b': _L0_ffn_in['b'], 'L1_xattn_w_q': _L1_xattn_in['w_q'], 'L1_xattn_b_q': _L1_xattn_in['b_q'], 'L1_xattn_w_k': _L1_xattn_in['w_k'], 'L1_xattn_b_k': _L1_xattn_in['b_k'], 'L1_xattn_w_v': _L1_xattn_in['w_v'], 'L1_xattn_b_v': _L1_xattn_in['b_v'], 'L1_xattn_w_o': _L1_xattn_in['w_o'], 'L1_xattn_b_o': _L1_xattn_in['b_o'], 'L1_ffn_Wg': _L1_ffn_in['Wg'], 'L1_ffn_bg': _L1_ffn_in['bg'], 'L1_ffn_W1': _L1_ffn_in['W1'], 'L1_ffn_b1': _L1_ffn_in['b1'], 'L1_ffn_W2': _L1_ffn_in['W2'], 'L1_ffn_b2': _L1_ffn_in['b2']}

def reference(x, ctx_768, mask_BxS_bf1, mask_BxS2_bf1, g_xattn, g_ffn, L0_xattn_Wq, L0_xattn_Wk, L0_xattn_Wv, L0_xattn_W_film_in, L0_xattn_b_film_in, L0_xattn_W_film_out, L0_xattn_b_film_out, L0_xattn_g_norm_in, L0_xattn_b_norm_in, L0_xattn_g_norm_out, L0_xattn_b_norm_out, L0_xattn_g_ffn, L0_xattn_b_ffn, L0_xattn_W1, L0_xattn_b1, L0_xattn_W2, L0_xattn_b2, L0_xattn_log_dt, L0_xattn_A_re, L0_xattn_A_im, L0_xattn_C_re, L0_xattn_C_im, L0_xattn_D_skip, L0_xattn_mod_gate, L0_ffn_wg, L0_ffn_W, L0_ffn_b, L1_xattn_w_q, L1_xattn_b_q, L1_xattn_w_k, L1_xattn_b_k, L1_xattn_w_v, L1_xattn_b_v, L1_xattn_w_o, L1_xattn_b_o, L1_ffn_Wg, L1_ffn_bg, L1_ffn_W1, L1_ffn_b1, L1_ffn_W2, L1_ffn_b2):
    import jax
    import jax.numpy as jnp

    def _L0_xattn_ref(x_text, x_vision, text_mask, vision_mask, Wq, Wk, Wv, W_film_in, b_film_in, W_film_out, b_film_out, g_norm_in, b_norm_in, g_norm_out, b_norm_out, g_ffn, b_ffn, W1, b1, W2, b2, log_dt, A_re, A_im, C_re, C_im, D_skip, mod_gate):
        import jax, jax.numpy as jnp
        import numpy as np
        B, T, DT, G, DV = (16, 64, 128, 72, 96)
        H, DH = (4, 32)
        INNER = H * DH
        HID = 4 * DT
        N_STATE = 64
        K_TOP = 32

        def layernorm(x, g, b, eps=1e-05):
            m = x.mean(-1, keepdims=True)
            v = x.var(-1, keepdims=True)
            return (x - m) * jax.lax.rsqrt(v + eps) * g + b

        def s4d(x, log_dt, A_re, A_im, C_re, C_im, D_skip):
            Bb, L, D = x.shape
            dt = jnp.exp(log_dt)
            A = A_re + 1j * A_im
            C = C_re + 1j * C_im
            dtA = dt[:, None] * A
            dC = C * (jnp.exp(dtA) - 1.0) / A
            powers = jnp.exp(dtA[:, :, None] * jnp.arange(L))
            K = 2.0 * jnp.einsum('dn,dnl->dl', dC, powers).real
            n = 2 * L
            Kf = jnp.fft.rfft(K, n=n, axis=-1)
            xf = jnp.fft.rfft(x, n=n, axis=1)
            y = jnp.fft.irfft(xf * Kf.T[None], n=n, axis=1)[:, :L]
            return y + x * D_skip
        Bb, Tt, D = x_text.shape
        Gg = x_vision.shape[1]
        Q = (x_text @ Wq).reshape(Bb, Tt, H, DH)
        K = (x_vision @ Wk).reshape(Bb, Gg, H, DH)
        scores = jnp.einsum('bthd,bghd->bhtg', Q, K) / np.sqrt(DH).astype(np.float32)
        scores = jnp.where(vision_mask[:, None, None, :], scores, -jnp.inf)
        topv, topi = jax.lax.top_k(scores, K_TOP)
        probs = jax.nn.softmax(topv, axis=-1)
        bi = jnp.arange(Bb)[:, None, None, None]
        hi = jnp.arange(H)[None, :, None, None]
        ti = jnp.arange(Tt)[None, None, :, None]
        attn = jnp.zeros_like(scores).at[bi, hi, ti, topi].set(probs)
        attn_mean = attn.mean(axis=1)
        V = x_vision @ Wv
        c_t = jnp.einsum('btg,bgd->btd', attn_mean, V)
        c_t = c_t * text_mask[..., None]
        x = layernorm(x_text, g_norm_in, b_norm_in)
        scale_in, shift_in = jnp.split(c_t @ W_film_in + b_film_in, 2, axis=-1)
        x = x * (1.0 + mod_gate * scale_in) + mod_gate * shift_in
        y = s4d(x, log_dt, A_re, A_im, C_re, C_im, D_skip)
        scale_out, shift_out = jnp.split(c_t @ W_film_out + b_film_out, 2, axis=-1)
        y = y * (1.0 + mod_gate * scale_out) + mod_gate * shift_out
        xt = x_text + y
        h = layernorm(xt, g_ffn, b_ffn)
        h = jax.nn.gelu(h @ W1 + b1, approximate=False) @ W2 + b2
        xt = xt + h
        return layernorm(xt, g_norm_out, b_norm_out)

    def _L0_ffn_ref(x, wg, W, b):
        import jax, jax.numpy as jnp
        import numpy as np
        H = 128
        E = 8
        B, S = (4, 256)
        Bb, Ss, Hh = x.shape
        Ee = wg.shape[1]
        T = Bb * Ss
        C = T // Ee
        xt = x.reshape(T, Hh)
        logits = xt @ wg
        probs = jax.nn.softmax(logits, axis=-1)
        idx = jnp.argmax(probs, axis=-1)
        mask = jax.nn.one_hot(idx, Ee, dtype=xt.dtype)
        locations = jnp.cumsum(mask, axis=0) - mask
        mask = mask * (locations < C).astype(xt.dtype)
        gate = jnp.sum(probs * mask, axis=-1)
        loc_s = jnp.sum(locations * mask, axis=-1).astype(jnp.int32)
        loc_oh = jax.nn.one_hot(loc_s, C, dtype=xt.dtype)
        dispatch = mask[:, :, None] * loc_oh[:, None, :]
        combine = gate[:, None, None] * dispatch
        exp_in = jnp.einsum('tec,th->ech', dispatch, xt)
        exp_out = jnp.einsum('ech,efh->ecf', exp_in, W) + b[:, None, :]
        out = jnp.einsum('tec,ecf->tf', combine, exp_out)
        return out.reshape(Bb, Ss, Hh)

    def _L1_xattn_ref(x, context, w_q, b_q, w_k, b_k, w_v, b_v, w_o, b_o):
        import jax, jax.numpy as jnp
        import numpy as np
        N_HEADS = 16
        DIMS = 128
        D_CTX = 96
        HEAD = DIMS // N_HEADS
        B, Lq, D = x.shape
        q = x @ w_q + b_q
        k = context @ w_k + b_k
        v = context @ w_v + b_v
        q = q.reshape(B, Lq, N_HEADS, HEAD)
        k = k.reshape(B, -1, N_HEADS, HEAD)
        v = v.reshape(B, -1, N_HEADS, HEAD)
        scale = 1.0 / np.sqrt(HEAD).astype(np.float32)
        scores = jnp.einsum('bqhd,bkhd->bhqk', q, k) * scale
        weights = jax.nn.softmax(scores, axis=-1)
        out = jnp.einsum('bhqk,bkhd->bqhd', weights, v).reshape(B, Lq, D)
        return out @ w_o + b_o

    def _L1_ffn_ref(x, Wg, bg, W1, b1, W2, b2):
        import jax, jax.numpy as jnp
        import numpy as np
        B, T, D, H, E = (4, 256, 128, 512, 8)
        gate_scores = x @ Wg + bg
        top1 = jnp.argmax(gate_scores, axis=-1)
        onehot = jax.nn.one_hot(top1, Wg.shape[-1], dtype=x.dtype)
        h = jax.nn.relu(jnp.einsum('btd,edh->beth', x, W1) + b1[None, :, None, :])
        y = jnp.einsum('beth,ehd->betd', h, W2) + b2[None, :, None, :]
        out = jnp.einsum('betd,bte->btd', y, onehot)
        return out
    x = x + jnp.tanh(g_xattn[0]) * _L0_xattn_ref(_layernorm(x, axis=-1), ctx_768, mask_BxS_bf1, mask_BxS2_bf1, L0_xattn_Wq, L0_xattn_Wk, L0_xattn_Wv, L0_xattn_W_film_in, L0_xattn_b_film_in, L0_xattn_W_film_out, L0_xattn_b_film_out, L0_xattn_g_norm_in, L0_xattn_b_norm_in, L0_xattn_g_norm_out, L0_xattn_b_norm_out, L0_xattn_g_ffn, L0_xattn_b_ffn, L0_xattn_W1, L0_xattn_b1, L0_xattn_W2, L0_xattn_b2, L0_xattn_log_dt, L0_xattn_A_re, L0_xattn_A_im, L0_xattn_C_re, L0_xattn_C_im, L0_xattn_D_skip, L0_xattn_mod_gate)
    x = x + jnp.tanh(g_ffn[0]) * _L0_ffn_ref(_layernorm(x, axis=-1), L0_ffn_wg, L0_ffn_W, L0_ffn_b)
    x = x + jnp.tanh(g_xattn[1]) * _L1_xattn_ref(_layernorm(x, axis=-1), ctx_768, L1_xattn_w_q, L1_xattn_b_q, L1_xattn_w_k, L1_xattn_b_k, L1_xattn_w_v, L1_xattn_b_v, L1_xattn_w_o, L1_xattn_b_o)
    x = x + jnp.tanh(g_ffn[1]) * _L1_ffn_ref(_layernorm(x, axis=-1), L1_ffn_Wg, L1_ffn_bg, L1_ffn_W1, L1_ffn_b1, L1_ffn_W2, L1_ffn_b2)
    return x

_drawn_inputs = setup_inputs


def setup_inputs(seed=0):
    import zlib

    import numpy as np

    out = dict(_drawn_inputs(seed))
    spreads = {'g_ffn': (-1.0, 0.6),
     'L0_xattn_b_film_in': (0.0, 0.1),
     'L0_xattn_b_film_out': (0.0, 0.1),
     'L0_xattn_g_norm_in': (1.0, 0.2),
     'L0_xattn_b_norm_in': (0.0, 0.1),
     'L0_xattn_g_norm_out': (1.0, 0.2),
     'L0_xattn_b_norm_out': (0.0, 0.1),
     'L0_xattn_g_ffn': (1.0, 0.6),
     'L0_xattn_b_ffn': (0.0, 0.453),
     'L0_xattn_b1': (0.0, 0.1),
     'L0_xattn_b2': (0.0, 0.1),
     'L0_xattn_A_re': (-0.5, 0.2)}
    factors = {'L0_ffn_b': 3.501,
     'L1_xattn_b_q': 6.606,
     'L1_xattn_b_k': 8.0,
     'L1_ffn_b1': 8.0,
     'L1_ffn_b2': 8.0}
    for name, (base, spread) in spreads.items():
        noise = np.random.default_rng([zlib.crc32(name.encode()), seed]).standard_normal(out[name].shape)
        drawn = base * np.exp(spread * noise) if base else spread * noise
        out[name] = jnp.asarray(drawn.astype(out[name].dtype))
    for name, factor in factors.items():
        out[name] = (out[name] * factor).astype(out[name].dtype)
    return out
```

```python
from contextlib import ExitStack

import numpy as np
import concourse.bass as bass
from concourse import mybir

F32 = mybir.dt.float32
BF16 = mybir.dt.bfloat16
U8 = mybir.dt.uint8
ALU = mybir.AluOpType
ACT = mybir.ActivationFunctionType
AX = mybir.AxisListType

P = 128
B, S, D = 16, 256, 128
T = B * S // P
QT = S // P
NK, C = 1601, 96
KT = -(-NK // P)
TAIL = NK - (KT - 1) * P
H0, DH0, TOPK = 4, 32, 32
NST, L = 64, S
H1, DH1 = 16, 8
E = 8
CAP = B * S // E
HID = 4 * D
EPS = 1e-5
BIG = 1e30
GONE = -3e38
GT = 4
NG = T // GT
PICK = 51
PIECES = [(c, min(PICK, NK - c)) for c in range(0, NK, PICK)]
CHUNKS = [(c, min(512, NK - c)) for c in range(0, NK, 512)]


def kn(kt):
    return P if kt < KT - 1 else TAIL


def over(ap, n):
    return ap.unsqueeze(2).to_broadcast([ap.shape[0], ap.shape[1], n])


def rows(ap, n):
    return ap.unsqueeze(1).to_broadcast([ap.shape[0], n, ap.shape[1]])


class Steps:

    def __init__(self, eng, sem):
        self.eng, self.sem, self.n = eng, sem, 0

    def add(self, ins):
        ins.then_inc(self.sem, 1)
        self.n += 1
        return ins

    def after(self):
        if self.n:
            self.eng.wait_ge(self.sem, self.n)

    def link(self, ins):
        self.add(ins)
        self.after()
        return ins

    def restart(self):
        self.after()
        self.eng.sem_clear(self.sem)
        self.n = 0


def setup_phase(nc, a, k):
    with ExitStack() as ctx:
        def sb(name, shape, dt=F32):
            return ctx.enter_context(nc.sbuf_tensor(name, shape, dt))

        sems = []

        def sem(name):
            sems.append(ctx.enter_context(nc.semaphore(name)))
            return sems[-1]

        wq, wk, wv = sb("wq", [P, D]), sb("wk", [C, D]), sb("wv", [C, D])
        film = sb("film", [P, 4 * D])
        wqT = sb("wqT", [P, D])
        wkT = sb("wkT", [P, C])
        wvT = sb("wvT", [P, C])
        par_d = sb("par_d", [P, 4, 2, NST])
        par = sb("par", [P, 4, D])
        dt_b = sb("dt_b", [P, D])
        re, im = sb("re", [P, D]), sb("im", [P, D])
        lrow = sb("lrow", [P, 32])
        NA = 48 * D + 3 * D
        arg = sb("arg", [P, NA])
        turns = sb("turns", [P, NA])
        mag = sb("mag", [P, D, 32])
        pm, qm = sb("pm", [P, D]), sb("qm", [P, D])
        w = [sb(f"w{i}", [P, D]) for i in range(10)]
        gtab, ztab = sb("gtab", [P, D, 16]), sb("ztab", [P, D, 16])
        kblk = sb("kblk", [P, 16, P])
        wraw = sb("wraw", [P, E, D])
        krow = sb("krow", [P, 3 * P])
        dskip = sb("dskip", [P, 1])
        m8 = sb("m8", [B, NK], U8)
        mf = sb("mf", [B, NK])
        sq = sb("sq", [P, T, D])
        mean, var, rstd = sb("mean", [P, T]), sb("var", [P, T]), sb("rstd", [P, T])
        mhalf = k.mhalf
        tm8, tmf = sb("tm8", [T, P], U8), sb("tmf", [T, P])
        gates = sb("gates", [P, 4])
        ph1, ph2, sgn = sb("ph1", [P, 1]), sb("ph2", [P, 1]), sb("sgn", [P, 1])
        modg = sb("modg", [P, 1])
        gin, bin_ = sb("gin", [P, D]), sb("bin", [P, D])
        ps = [ctx.enter_context(nc.psum_tensor(f"ps_s{i}", [P, 512], F32)) for i in range(8)]
        X, X0, XF, ident = k.X, k.X0, k.XF, k.ident

        in_w, in_par, in_x, in_row = sem("in_w"), sem("in_par"), sem("in_x"), sem("in_row")
        in_mask, in_g = sem("in_mask"), sem("in_g")
        consts, pool_step, dve_step = sem("consts"), sem("pool_step"), sem("dve_step")
        tr_done, tr_out, wfold, table_k = sem("tr_done"), sem("tr_out"), sem("wfold"), sem("table_k")
        dt_done, args_done, sins_done, mags_done = sem("dt_done"), sem("args_done"), sem("sins_done"), sem("mags_done")
        tanh_done, tables, kb_out = sem("tanh_done"), sem("tables"), sem("kb_out")
        mask_done, scr, k_back, kpad_done = sem("mask_done"), sem("scr"), sem("k_back"), sem("kpad_done")
        centred, squared, var_done, rstd_done, fold_out = (sem("centred"), sem("squared"), sem("var_done"),
                                                           sem("rstd_done"), sem("fold_out"))
        tmask_done = sem("tmask_done")
        phase = ExitStack()
        block = phase.enter_context(nc.Block())

        @block.sync
        def _(sp):
            for dst, src in ((wq[:, :], a["L0_xattn_Wq"]), (wk[:, :], a["L0_xattn_Wk"]), (wv[:, :], a["L0_xattn_Wv"]),
                             (film[:, 0:2 * D], a["L0_xattn_W_film_in"]),
                             (film[:, 2 * D:4 * D], a["L0_xattn_W_film_out"]),
                             (wraw[:, :, :], a["L0_ffn_W"].rearrange("e f h -> f e h"))):
                sp.dma_start(dst, src).then_inc(in_w, 16)
            for n, name in enumerate(("A_re", "A_im", "C_re", "C_im")):
                for c in range(2):
                    sp.dma_start(par_d[:, n, c, :], a["L0_xattn_" + name]).then_inc(in_par, 16)
            sp.dma_start(X[:, :, :], a["x"].rearrange("b (h p) d -> p (b h) d", p=P)).then_inc(in_x, 16)
            sp.dma_start(m8[:, :], a["mask_BxS2_bf1"]).then_inc(in_mask, 16)
            sp.dma_start(tm8[:, :], a["mask_BxS_bf1"].rearrange("b (h p) -> (b h) p", p=P)).then_inc(in_mask, 16)
            for dst, src in k.later_loads(a):
                sp.dma_start(dst, src).then_inc(in_g, 16)
            sp.wait_ge(mask_done, 1)
            sp.dma_start(k.maskrow[:, :], mf[:, :]).then_inc(scr, 16)
            sp.wait_ge(kb_out, 4)
            for j in range(8):
                sp.dma_start(k.kern.rearrange("(c j) (p b) -> j p c b", j=8, b=16)[j],
                             kblk[16 * j:16 * j + 16, :, 16 * j:16 * j + 16]).then_inc(scr, 16)
            sp.wait_ge(scr, 16 * 9)
            sp.dma_start(krow[:, P:3 * P], k.kern[:, :]).then_inc(k_back, 16)
            sp.wait_ge(kpad_done, 1)
            sp.dma_start(k.kernpad[:, :], krow[:, :]).then_inc(scr, 16)
            sp.wait_ge(scr, 16 * 10)
            sp.wait_ge(in_g, 16 * len(k.later_loads(a)))

        @block.gpsimd
        def _(pool):
            g = nc.gpsimd
            st = Steps(pool, pool_step)
            for dst, name in ((gin, "L0_xattn_g_norm_in"), (bin_, "L0_xattn_b_norm_in"), (dt_b, "L0_xattn_log_dt")):
                pool.dma_start(dst[:, :], a[name].partition_broadcast(P)).then_inc(in_row, 16)
            pool.dma_start(modg[:, :], a["L0_xattn_mod_gate"].partition_broadcast(P)).then_inc(in_row, 16)
            for i, name in enumerate(("g_xattn", "g_ffn")):
                pool.dma_start(gates[:, 2 * i:2 * i + 2], a[name].partition_broadcast(P)).then_inc(in_row, 16)
            pool.dma_start(dskip[:, :], a["L0_xattn_D_skip"].unsqueeze(1)).then_inc(in_row, 16)
            for i, name in enumerate(("in", "out")):
                pool.dma_start(k.WVF[C:C + 1, 2 * D * i:2 * D * i + 2 * D],
                               a["L0_xattn_b_film_" + name].unsqueeze(0)).then_inc(in_row, 16)
            st.link(g.memset(ident[:, :], 0.0))
            st.link(g.affine_select(out=ident[:, :], in_=ident[:, :], compare_op=ALU.not_equal, fill=1.0, base=0,
                                    pattern=[[-1, P]], channel_multiplier=1))
            pool.sem_inc(consts, 1)
            for half in range(2):
                st.link(g.iota(lrow[:, 16 * half:16 * half + 16], [[1 if half == 0 else 16, 16]], base=0,
                               channel_multiplier=0, allow_small_or_imprecise_dtypes=True))
            for t, lo, hi in ((ph1, np.pi / 2, 0.0), (ph2, 0.0, np.pi / 2), (sgn, 2.0, -2.0)):
                st.link(g.memset(t[0:NST, :], float(lo)))
                st.link(g.memset(t[NST:P, :], float(hi)))
            st.link(g.memset(mhalf[:, :], -0.5))
            st.link(g.memset(krow[:, 0:P], 0.0))
            st.link(g.memset(k.ones[:, :], 1.0))
            st.link(g.memset(k.wv1[C:C + 2, :], 0.0))
            pool.sem_inc(consts, 1)
            pool.dma_start(k.wv1[C + 1:C + 2, :], a["L1_xattn_b_v"].unsqueeze(0)).then_inc(in_row, 16)
            for n in range(2):
                pool.wait_ge(var_done, n + 1)
                g.tensor_tensor(rstd[:, :], var[:, :], mhalf[:, :], ALU.pow).then_inc(rstd_done, 1)

        @block.tensor
        def _(pe):
            pe.wait_ge(in_w, 16 * 6)
            pe.wait_ge(in_par, 16 * 8)
            pe.wait_ge(consts, 1)
            nc.tensor.transpose(ps[0][:, 0:P], wq[:, :], ident[:, :])
            nc.tensor.transpose(ps[0][:, P:P + C], wk[:, :], ident[0:C, 0:C])
            nc.tensor.transpose(ps[0][:, 2 * P:2 * P + C], wv[:, :], ident[0:C, 0:C]).then_inc(tr_done, 1)
            for n in range(4):
                ins = nc.tensor.transpose(ps[1][:, n * P:n * P + P], par_d[:, n, :, :].rearrange("p c n -> p (c n)"),
                                          ident[:, :])
            ins.then_inc(tr_done, 1)
            pe.wait_ge(tmask_done, 1)
            nc.tensor.transpose(ps[2][:, H0 * C:H0 * C + T], tmf[:, :], ident[0:T, 0:T]).then_inc(tr_done, 1)
            pe.wait_ge(tr_out, 4)
            for e in range(E):
                ins = nc.tensor.transpose(ps[e // 4][:, (e % 4) * P:(e % 4) * P + P], wraw[:, e, :], ident[:, :])
            ins.then_inc(tr_done, 1)
            pe.wait_ge(fold_out, 1)
            for h in range(H0):
                nc.tensor.matmul(ps[2][:, h * C:(h + 1) * C], wqT[DH0 * h:DH0 * h + DH0, :],
                                 wkT[DH0 * h:DH0 * h + DH0, :], start=True, stop=True).then_inc(wfold, 1)
                pe.wait_ge(wfold, h + 1)
            nc.tensor.matmul(ps[3][0:C, :], wvT[:, :], film[:, :], start=True, stop=True).then_inc(wfold, 1)
            pe.wait_ge(tables, 1)
            for c in range(16):
                ins = nc.tensor.matmul(ps[4 + c // 4][:, (c % 4) * P:(c % 4) * P + P],
                                       gtab[:, 8 * c:8 * c + 8, :].rearrange("p d a -> p (d a)"),
                                       ztab[:, 8 * c:8 * c + 8, :].rearrange("p d a -> p (d a)"), start=True, stop=True)
                if c % 4 == 3:
                    ins.then_inc(table_k, 1)

        @block.scalar
        def _(act):
            act.wait_ge(tr_done, 1)
            nc.scalar.copy(wqT[:, :], ps[0][:, 0:P]).then_inc(tr_out, 1)
            nc.scalar.copy(wkT[:, :], ps[0][:, P:P + C]).then_inc(tr_out, 1)
            nc.scalar.copy(wvT[:, :], ps[0][:, 2 * P:2 * P + C]).then_inc(tr_out, 1)
            act.wait_ge(tr_done, 2)
            nc.scalar.copy(par[:, :, :].rearrange("p a d -> p (a d)"), ps[1][:, :]).then_inc(tr_out, 1)
            act.wait_ge(tr_done, 3)
            nc.scalar.copy(k.tmask[:, :], ps[2][:, H0 * C:H0 * C + T]).then_inc(fold_out, 1)
            act.wait_ge(tr_done, 4)
            for n in range(2):
                nc.scalar.copy(k.wm0[:, 4 * n:4 * n + 4, :].rearrange("p e f -> p (e f)"), ps[n][:, :]
                               ).then_inc(tr_out, 1)
            act.wait_ge(in_row, 16 * 10)
            nc.scalar.activation(re[:, :], dt_b[:, :], ACT.Exp).then_inc(dt_done, 1)
            nc.scalar.activation(k.TG[:, :], gates[:, :], ACT.Tanh).then_inc(dt_done, 1)
            act.wait_ge(wfold, H0)
            nc.scalar.mul(k.G[:, :], ps[2][:, 0:H0 * C], DH0 ** -0.5).then_inc(fold_out, 1)
            act.wait_ge(wfold, H0 + 1)
            nc.scalar.activation(k.WVF[0:C, :], ps[3][0:C, :], ACT.Copy, scale=modg[0:C, 0:1]).then_inc(fold_out, 1)
            for n in range(2):
                act.wait_ge(centred, n + 1)
                nc.scalar.activation(sq[:, :, :], XF[:, :, :], ACT.Square).then_inc(squared, 1)
            act.wait_ge(args_done, 1)
            nc.scalar.activation(mag[:, :, :], mag[:, :, :], ACT.Exp).then_inc(mags_done, 1)
            nc.scalar.activation(w[0][:, :], re[:, :], ACT.Tanh, scale=0.5).then_inc(tanh_done, 1)
            act.wait_ge(args_done, 2)
            nc.scalar.activation(arg[:, :], arg[:, :], ACT.Sin).then_inc(sins_done, 1)
            for c in range(4):
                act.wait_ge(table_k, c + 1)
                nc.scalar.copy(kblk[:, 4 * c:4 * c + 4, :],
                               ps[4 + c][:, :].rearrange("p (c n) -> p c n", n=P)).then_inc(kb_out, 1)

        @block.vector
        def _(dve):
            v = nc.vector
            st = Steps(dve, dve_step)
            dve.wait_ge(in_mask, 32)
            st.link(v.tensor_copy(tmf[:, :], tm8[:, :]))
            v.tensor_scalar(tmf[:, :], tmf[:, :], 1.0 / H0, None, ALU.mult).then_inc(tmask_done, 1)
            st.link(v.tensor_copy(mf[:, :], m8[:, :]))
            v.tensor_scalar(mf[:, :], mf[:, :], BIG, -BIG, ALU.mult, ALU.add).then_inc(mask_done, 1)
            dve.wait_ge(in_g, 16 * len(k.later_loads(a)))
            st.link(v.tensor_scalar(k.bq1[:, :], k.bq1[:, :], DH1 ** -0.5, None, ALU.mult))
            dve.wait_ge(in_row, 16 * 10)
            brow = k.WVF[C:C + 1, :]
            st.link(v.tensor_scalar(brow, brow, modg[C:C + 1, 0:1], None, ALU.mult))
            for c in (0, 2):
                st.link(v.tensor_scalar(brow[:, c * D:(c + 1) * D], brow[:, c * D:(c + 1) * D], 1.0, None, ALU.add))

            def norm(src, dst, n):
                st.link(v.tensor_reduce(mean[:, :], src[:, :, :], AX.X, ALU.add))
                st.link(v.tensor_scalar(mean[:, :], mean[:, :], 1.0 / D, None, ALU.mult))
                st.link(v.tensor_tensor(XF[:, :, :], src[:, :, :], over(mean[:, :], D), ALU.subtract))
                dve.sem_inc(centred, 1)
                dve.wait_ge(squared, n + 1)
                st.link(v.tensor_reduce(var[:, :], sq[:, :, :], AX.X, ALU.add))
                v.tensor_scalar(var[:, :], var[:, :], 1.0 / D, EPS, ALU.mult, ALU.add).then_inc(var_done, 1)
                dve.wait_ge(rstd_done, n + 1)
                st.link(v.tensor_tensor(dst[:, :, :], XF[:, :, :], over(rstd[:, :], D), ALU.mult))

            dve.wait_ge(in_x, 16)
            norm(X, X0, 0)
            norm(X0, XF, 1)
            st.link(v.tensor_tensor(XF[:, :, :], XF[:, :, :], rows(gin[:, :], T), ALU.mult))
            st.add(v.tensor_tensor(XF[:, :, :], XF[:, :, :], rows(bin_[:, :], T), ALU.add))

            dve.wait_ge(dt_done, 2)
            dve.wait_ge(tr_out, 4)
            dve.wait_ge(consts, 2)
            a_re, a_im, c_re, c_im = (par[:, n, :] for n in range(4))
            st.link(v.tensor_tensor(im[:, :], re[:, :], a_im, ALU.mult))
            st.link(v.tensor_tensor(re[:, :], re[:, :], a_re, ALU.mult))
            lows = arg[:, 0:32 * D].rearrange("p (d l) -> p d l", l=32)
            highs = arg[:, 32 * D:48 * D].rearrange("p (d l) -> p d l", l=16)
            st.add(v.tensor_tensor(mag[:, :, :], over(re[:, :], 32), rows(lrow[:, :], D), ALU.mult))
            st.add(v.tensor_tensor(lows, over(im[:, :], 32), rows(lrow[:, :], D), ALU.mult))
            st.add(v.tensor_tensor(highs, over(im[:, :], 16), rows(lrow[:, 16:32], D), ALU.mult))
            ends = [32 * D, 48 * D, 49 * D, 50 * D, 51 * D]
            st.add(v.tensor_copy(arg[:, ends[1]:ends[2]], im[:, :]))
            st.add(v.tensor_copy(arg[:, ends[2]:ends[3]], im[:, :]))
            st.link(v.tensor_scalar(arg[:, ends[3]:ends[4]], im[:, :], 0.5, None, ALU.mult))
            dve.sem_inc(args_done, 1)
            phases = [(0, ends[0], ph1[:, 0:1]), (ends[0], ends[1], ph2[:, 0:1]), (ends[1], ends[2], np.pi / 2),
                      (ends[2], ends[4], 0.0)]
            magic = 1.5 * 2 ** 23
            tau = 2 * np.pi
            t1 = float(np.float32(6.28125))
            t2 = float(np.float32(np.round((tau - t1) * 2 ** 22) / 2 ** 22))
            t3 = float(np.float32(tau - t1 - t2))
            for lo, hi, ph in phases:
                st.add(v.tensor_scalar(turns[:, lo:hi], arg[:, lo:hi], ph if isinstance(ph, bass.AP) else float(ph),
                                       1.0 / tau, ALU.add, ALU.mult))
            st.after()
            st.link(v.tensor_scalar(turns[:, :], turns[:, :], magic, None, ALU.add))
            st.link(v.tensor_scalar(turns[:, :], turns[:, :], -magic, None, ALU.add))
            for t in (t1, t2, t3):
                st.link(v.scalar_tensor_tensor(out=arg[:, :], in0=turns[:, :], scalar=-t, in1=arg[:, :],
                                               op0=ALU.mult, op1=ALU.add))
            pi = float(np.nextafter(np.float32(np.pi), np.float32(0)))
            for lo, hi, ph in phases:
                st.add(v.tensor_scalar(arg[:, lo:hi], arg[:, lo:hi], ph if isinstance(ph, bass.AP) else float(ph),
                                       pi, ALU.add, ALU.min))
            st.after()
            st.link(v.tensor_scalar(arg[:, :], arg[:, :], -pi, None, ALU.max))
            dve.sem_inc(args_done, 1)
            dve.wait_ge(sins_done, 1)
            dve.wait_ge(tanh_done, 1)
            dve.wait_ge(mags_done, 1)
            cos_a, sin_a, sin_h = (arg[:, ends[i]:ends[i + 1]] for i in (1, 2, 3))

            def mul(o, x, y):
                st.link(v.tensor_tensor(o, x, y, ALU.mult))

            t, u, ex, er, ei, qr, qi, x1, x2, inv = (w[i][:, :] for i in range(10))
            st.link(v.tensor_scalar(u, t, -1.0, 1.0, ALU.mult, ALU.add))
            st.link(v.reciprocal(u, u))
            st.link(v.scalar_tensor_tensor(out=ex, in0=t, scalar=2.0, in1=u, op0=ALU.mult, op1=ALU.mult))
            mul(x1, sin_h, sin_h)
            mul(er, ex, cos_a)
            st.link(v.scalar_tensor_tensor(out=er, in0=x1, scalar=-2.0, in1=er, op0=ALU.mult, op1=ALU.add))
            st.link(v.scalar_tensor_tensor(out=ei, in0=ex, scalar=1.0, in1=sin_a, op0=ALU.add, op1=ALU.mult))

            def cmul(outr, outi, ar, ai, br, bi):
                mul(x1, ar, br)
                mul(x2, ai, bi)
                st.link(v.tensor_tensor(outr, x1, x2, ALU.subtract))
                mul(x1, ar, bi)
                mul(x2, ai, br)
                st.link(v.tensor_tensor(outi, x1, x2, ALU.add))

            cmul(qr, qi, c_re, c_im, er, ei)
            mul(x1, a_re, a_re)
            mul(x2, a_im, a_im)
            st.link(v.tensor_tensor(inv, x1, x2, ALU.add))
            st.link(v.reciprocal(inv, inv))
            st.link(v.tensor_scalar(u, a_im, -1.0, None, ALU.mult))
            cmul(er, ei, qr, qi, a_re, u)
            mul(er, er, inv)
            mul(ei, ei, inv)
            st.link(v.tensor_scalar(pm[:, :], er, sgn[:, 0:1], None, ALU.mult))
            st.link(v.tensor_scalar(qm[:, :], ei, -2.0, None, ALU.mult))
            st.add(v.tensor_tensor(ztab[:, :, :], lows[:, :, 0:16], mag[:, :, 0:16], ALU.mult))
            st.link(v.tensor_tensor(gtab[:, :, :], lows[:, :, 16:32], over(pm[:, :], 16), ALU.mult))
            st.link(v.tensor_tensor(highs, highs, over(qm[:, :], 16), ALU.mult))
            st.link(v.tensor_tensor(gtab[:, :, :], gtab[:, :, :], highs, ALU.add))
            v.tensor_tensor(gtab[:, :, :], gtab[:, :, :], mag[:, :, 16:32], ALU.mult).then_inc(tables, 1)
            dve.wait_ge(k_back, 16)
            v.tensor_tensor(krow[:, P:P + 1], krow[:, P:P + 1], dskip[:, 0:1], ALU.add).then_inc(kpad_done, 1)

        phase.close()
        with nc.Block() as clearing:
            @clearing.gpsimd
            def _(pool):
                for used in sems:
                    pool.sem_clear(used)


def attention0_phase(nc, a, k):
    NS = QT * H0
    with ExitStack() as ctx:
        def sb(name, shape, dt=F32):
            return ctx.enter_context(nc.sbuf_tensor(name, shape, dt))

        def sem(name):
            return ctx.enter_context(nc.semaphore(name))

        ctxn = [sb(f"ctxn{i}", [P, KT, C]) for i in range(2)]
        ctxT = [sb(f"ctxT{i}", [C + 2, NK]) for i in range(2)]
        xn = [sb(f"xn{i}", [P, QT, D]) for i in range(2)]
        xT = sb("xT", [P, S])
        qT = [sb(f"qT{i}", [C + 1, H0, S]) for i in range(2)]
        sc = [sb(f"sc{i}", [P, NK]) for i in range(4)]
        pr = [sb(f"pr{i}", [P, NK]) for i in range(NS)]
        prT = sb("prT", [P, KT, P])
        diag = [sb(f"diag{i}", [P, P]) for i in range(NS)]
        top = sb("top", [P, 4, TOPK])
        etop = sb("etop", [P, 2, TOPK])
        cand = [sb(f"cand{i}", [P, len(PIECES), 8]) for i in range(2)]
        cleft = sb("cleft", [P, len(PIECES), 8])
        rest = sb("rest", [P, 2])
        doubt = sb("doubt", [P, 2])
        doubts = sb("doubts", [1, 1], mybir.dt.int32)
        onecol = sb("onecol", [P, 1])
        negm, den = sb("negm", [P, NS]), sb("den", [P, NS])
        rden = sb("rden", [P, NS])
        uT = sb("uT", [C + 1, P])
        fs = sb("fs", [P, 4 * D])
        kf = sb("kf", [P, NK])
        kpart = sb("kpart", [P, NK], BF16)
        vs = sb("vs", [P, KT, D])
        scores = ctx.enter_context(nc.psum_tensor("scores", [P, 4 * 512], F32))
        misc = ctx.enter_context(nc.psum_tensor("misc", [P, 512], F32))
        tps = [ctx.enter_context(nc.psum_tensor(f"tps{i}", [P, 512], F32)) for i in range(2)]
        ups = tps[0]
        dps = ctx.enter_context(nc.psum_tensor("dps", [P, 512], F32))
        X0, XF, ident = k.X0, k.XF, k.ident

        ctx_in = [sem(f"ctx_in{i}") for i in range(2)]
        ready, xn_ready = sem("ready"), sem("xn_ready")
        scores_ready, scores_out = sem("scores_ready"), sem("scores_out")
        misc_ready, misc_out = sem("misc_ready"), sem("misc_out")
        negm_ready, exp_done, top_ready, den_done, pr_ready = (sem("negm_ready"), sem("exp_done"), sem("top_ready"),
                                                               sem("den_done"), sem("pr_ready"))
        rden_ready, diag_ready = sem("rden_ready"), sem("diag_ready")
        tps_ready, tps_out, ups_ready, ups_out = sem("tps_ready"), sem("tps_out"), sem("ups_ready"), sem("ups_out")
        film_used, film_saved, kparts_ready, kparts_saved, vs_saved = (sem("film_used"), sem("film_saved"), sem("kparts_ready"),
                                                           sem("kparts_saved"), sem("vs_saved"))
        doubt_ready, doubts_ready, general_step = sem("doubt_ready"), sem("doubts_ready"), sem("general_step")
        slot_begun, pool_passed = sem("slot_begun"), sem("pool_passed")
        dve_step, pool_step = sem("dve_step"), sem("pool_step")
        block = ctx.enter_context(nc.Block())

        PER = 17

        def prep_jobs(b, what):
            n = {"ctx": 4, "x": 1, "q": 2, "k": 4, "v": 4}[what]
            if first_batch(b):
                lo = {"ctx": 0, "x": 4, "q": 5, "k": 10, "v": 18}[what]
                return lo, lo + n
            lo = {"ctx": -3, "x": -11, "q": -10, "k": 9, "v": 18}[what]
            if isinstance(b, int) and b == 1 and what in ("x", "q"):
                lo += 1
            if isinstance(b, int) and b == B - 1:
                lo -= {"k": 3, "v": 7}.get(what, 0)
            return PER * b + lo, PER * b + lo + n

        def film_job(tile, b, last=False):
            return PER * b + ((10 if last else 13) if tile else 5)

        LAST_FILMS = PER * (B - 1) + 15
        TPG = 4
        HALVES = ((0, 1), (2, 3))
        GROUPS = {1: (0,), 2: (1, 2), 3: (3,)}

        def first_batch(b):
            return isinstance(b, int) and b == 0

        def walk(eng, step):
            step(0, 0, 1, True, False)
            with eng.Fori(0, (B - 2) // 2) as i:
                step(2 * i + 1, 1, i + 2, False, False)
                step(2 * i + 2, 0, i + 2, False, False)
            step(B - 1, 1, None, False, True)

        @block.sync
        def _(sp):
            def load(b, par):
                if not first_batch(b) and not (isinstance(b, int) and b == 1):
                    sp.wait_ge(ups_ready, QT * (b - 1))
                n = a["ctx_768"]
                sp.dma_start(ctxn[par][:, 0:KT - 1, :],
                             n[bass.ds(b, 1), 0:(KT - 1) * P, :].rearrange("o (n p) d -> p (o n) d", p=P)
                             ).then_inc(ctx_in[par], 16)
                sp.dma_start(ctxn[par][0:TAIL, KT - 1, :],
                             n[bass.ds(b, 1), (KT - 1) * P:NK, :].rearrange("o p d -> (o p) d")
                             ).then_inc(ctx_in[par], 16)
                sp.dma_start(ctxT[par][C:C + 1, :], k.maskrow[bass.ds(b, 1), :]).then_inc(ctx_in[par], 16)

            def step(b, par, visit, first, last):
                if not last:
                    load(b + 1, 1 - par)
                for n in range(3):
                    sp.wait_ge(kparts_ready, 3 * b + n + 1)
                    sp.dma_start(k.keys[bass.ds(b, 1), n, :, :].rearrange("o p c -> (o p) c"),
                                 kpart[:, :]).then_inc(kparts_saved, 16)
                sp.wait_ge(misc_out, prep_jobs(b, "v")[1])
                sp.dma_start(k.values[bass.ds(b, 1), :, :].rearrange("o p c -> (o p) c"),
                             vs[:, :, :].rearrange("p n d -> p (n d)")).then_inc(vs_saved, 16)

            sp.wait_ge(ready, 1)
            load(0, 0)
            walk(sp, step)
            sp.wait_ge(kparts_saved, 16 * 3 * B)
            sp.wait_ge(vs_saved, 16 * B)

        @block.gpsimd
        def _(pool):
            g = nc.gpsimd
            st = Steps(pool, pool_step)
            for t in ctxT:
                st.link(g.memset(t[C:C + 2, :], 1.0))
            for t in qT:
                st.link(g.memset(t[C:C + 1, :, :], 1.0))
            st.link(g.memset(uT[C:C + 1, :], 1.0))
            st.link(g.memset(onecol[:, :], 1.0))
            st.link(g.memset(vs[64:P, KT - 1, :], 0.0))
            pool.sem_inc(ready, 1)

            def copy_x(b, par):
                st.link(g.tensor_copy(xn[par][:, :, :], X0[:, bass.ds(b * QT, QT), :]))
                pool.sem_inc(xn_ready, 1)

            def make_diag(b, s, first):
                pool.wait_ge(rden_ready, NS * b + s + 1)
                if not first and s < NS - 2:
                    pool.wait_ge(tps_ready, TPG * (QT * (b - 1) + s // H0 + 1))
                pool.sem_inc(pool_passed, 1)
                g.tensor_scalar(diag[s][:, :], ident[:, :], rden[:, s:s + 1], None, ALU.mult).then_inc(diag_ready, 1)

            def film(t, job):
                pool.wait_ge(misc_out, job + 1)
                x = XF[:, bass.ds(t, 1), :].rearrange("p o d -> p (o d)")
                st.link(g.tensor_tensor(x, x, fs[:, 0:D], ALU.mult))
                st.link(g.tensor_tensor(x, x, fs[:, D:2 * D], ALU.add))
                pool.dma_start(k.film_out[bass.ds(t, 1), :, :].rearrange("o p d -> (o p) d"), fs[:, 2 * D:4 * D]
                               ).then_inc(film_saved, 16)
                pool.sem_inc(film_used, 1)

            def split_keys(b):
                pool.wait_ge(misc_out, prep_jobs(b, "k")[1])
                for n in range(3):
                    if n or not first_batch(b):
                        pool.wait_ge(kparts_saved, 48 * b + 16 * n)
                    pool.sem_inc(pool_passed, 1)
                    st.link(g.tensor_copy(kpart[:, :], kf[:, :]))
                    pool.sem_inc(kparts_ready, 1)
                    if n < 2:
                        st.link(g.tensor_tensor(kf[:, :], kf[:, :], kpart[:, :], ALU.subtract))

            copy_x(0, 0)
            st.restart()

            def step(b, par, visit, first, last):
                for s in range(NS):
                    if s == 0 and not last:
                        copy_x(b + 1, 1 - par)
                    if not (first and s < 2):
                        make_diag(b if s >= 2 else b - 1, (s - 2) % NS, first)
                    if s == 0 and not first:
                        film(QT * (b - 1), film_job(0, b))
                    if s == 3:
                        split_keys(b)
                    if s == 4 and not first:
                        film(QT * b - 1, film_job(1, b, last))
                st.restart()

            walk(pool, step)
            for s in (NS - 2, NS - 1):
                make_diag(B - 1, s, False)
            for n in range(QT):
                film(T - QT + n, LAST_FILMS + n)
            pool.wait_ge(film_saved, 16 * T)

        @block.tensor
        def _(pe):
            t = nc.tensor

            def misc_job(job):
                if not (isinstance(job, int) and job == 0):
                    pe.wait_ge(misc_out, job)

            def prep_ctx(b, par, visit, groups):
                if groups[0] == 0:
                    pe.wait_ge(ctx_in[par], 48 * visit)
                for g in groups:
                    misc_job(prep_jobs(b, "ctx")[0] + g)
                    for kt in range(4 * g, min(4 * g + 4, KT)):
                        ins = t.transpose(misc[0:C, (kt % 4) * P:(kt % 4) * P + kn(kt)], ctxn[par][0:kn(kt), kt, :],
                                          ident[0:kn(kt), 0:kn(kt)])
                    ins.then_inc(misc_ready, 1)

            def prep_queries(b, par):
                job = prep_jobs(b, "x")[0]
                misc_job(job)
                pe.wait_ge(xn_ready, b + 1)
                for h in range(QT):
                    ins = t.transpose(misc[:, h * P:h * P + P], xn[par][:, h, :], ident[:, :])
                ins.then_inc(misc_ready, 1)
                for g in range(2):
                    misc_job(job + 1 + g)
                    for h in range(2 * g, 2 * g + 2):
                        ins = t.matmul(misc[0:C, (h % 2) * S:(h % 2) * S + S], k.G[:, h * C:(h + 1) * C], xT[:, :],
                                       start=True, stop=True)
                    ins.then_inc(misc_ready, 1)

            def prep_keys(b, par, groups):
                for g in groups:
                    c, n = CHUNKS[g]
                    misc_job(prep_jobs(b, "k")[0] + g)
                    t.matmul(misc[:, 0:n], k.wk1[:, :], ctxT[par][0:C, c:c + n],
                             start=True, stop=True).then_inc(misc_ready, 1)

            def prep_values(b, par, groups):
                for g in groups:
                    misc_job(prep_jobs(b, "v")[0] + g)
                    for kt in range(4 * g, min(4 * g + 4, KT)):
                        ins = t.matmul(misc[0:kn(kt), (kt % 4) * P:(kt % 4) * P + P],
                                       ctxT[par][:, kt * P:kt * P + kn(kt)], k.wv1[:, :], start=True, stop=True)
                    ins.then_inc(misc_ready, 1)

            def scores_of(b, par, s, j):
                if s == 0:
                    pe.wait_ge(misc_out, prep_jobs(b, "q" if first_batch(b) else "ctx")[1])
                if not (isinstance(j, int) and j == 0):
                    pe.wait_ge(scores_out, j)
                q = qT[par][:, s % H0, (s // H0) * P:(s // H0) * P + P]
                for c, n in CHUNKS:
                    ins = t.matmul(scores[:, c:c + n], q, ctxT[par][0:C + 1, c:c + n], start=True, stop=True)
                ins.then_inc(scores_ready, 1)

            def transpose_probs(tile, s0, jobs, groups):
                if groups[0] == 0:
                    pe.wait_ge(pr_ready, jobs)
                    pe.wait_ge(diag_ready, jobs)
                    if not (isinstance(tile, int) and tile == 0):
                        pe.wait_ge(ups_out, tile)
                for g in groups:
                    if not (isinstance(tile, int) and tile == 0 and g < 2):
                        pe.wait_ge(tps_out, TPG * tile + g - 1)
                    for kt in range(4 * g, min(4 * g + 4, KT)):
                        for h in range(H0):
                            ins = t.matmul(tps[g % 2][0:kn(kt), (kt % 4) * P:(kt % 4) * P + P],
                                           pr[s0 + h][:, kt * P:kt * P + kn(kt)], diag[s0 + h][:, :],
                                           start=(h == 0), stop=(h == H0 - 1))
                    ins.then_inc(tps_ready, 1)

            def times_ctx(tile, par):
                pe.wait_ge(tps_out, TPG * tile + TPG)
                for kt in range(KT):
                    ins = t.matmul(ups[0:C, 0:P], ctxn[par][0:kn(kt), kt, :], prT[0:kn(kt), kt, :],
                                   start=(kt == 0), stop=(kt == KT - 1))
                ins.then_inc(ups_ready, 1)

            def film(tile, job):
                pe.wait_ge(ups_out, tile + 1)
                misc_job(job)
                t.matmul(misc[:, :], uT[:, :], k.WVF[:, :], start=True, stop=True).then_inc(misc_ready, 1)

            def count_doubts(s, j):
                pe.wait_ge(doubt_ready, j + 1)
                if not isinstance(j, int) or j > 0:
                    pe.wait_ge(pr_ready, j)
                t.matmul(dps[0:1, 0:1], doubt[:, s % 2:s % 2 + 1], onecol[:, :], start=True, stop=True).then_inc(doubts_ready, 1)

            pe.wait_ge(ready, 1)
            prep_ctx(0, 0, 1, range(4))
            prep_queries(0, 0)
            scores_of(0, 0, 0, 0)
            scores_of(0, 0, 1, 1)

            def step(b, par, visit, first, last):
                for s in range(NS):
                    if not (first and s == 0):
                        count_doubts((s - 1) % NS, NS * b + s - 1)
                    if s < NS - 2:
                        scores_of(b, par, s + 2, NS * b + s + 2)
                    elif not last:
                        scores_of(b + 1, 1 - par, s + 2 - NS, NS * b + s + 2)
                    if s in GROUPS and not first:
                        transpose_probs(QT * b - 1, H0, NS * b, GROUPS[s])
                    if s == 3 and not first:
                        times_ctx(QT * b - 1, 1 - par)
                    if s - H0 in GROUPS:
                        transpose_probs(QT * b, 0, NS * b + H0, GROUPS[s - H0])
                    if s == 7:
                        times_ctx(QT * b, par)
                    if s in (0, 4) and not first:
                        film(QT * b - (QT if s == 0 else 1), film_job(s // H0, b, last))
                    if s in (1, 2):
                        prep_keys(b, par, HALVES[s - 1])
                    if s == 0 and not last:
                        prep_queries(b + 1, 1 - par)
                    if s in (6, 7):
                        prep_values(b, par, HALVES[s - 6])
                    if s in (4, 5) and not last:
                        prep_ctx(b + 1, 1 - par, visit, HALVES[s - 4])

            walk(pe, step)
            count_doubts(NS - 1, NS * B - 1)
            for n in range(QT):
                if n:
                    transpose_probs(T - 1, H0, NS * B, range(TPG))
                    times_ctx(T - 1, 1)
                film(T - QT + n, LAST_FILMS + n)

        @block.scalar
        def _(act):
            s_ = nc.scalar

            def misc_job(job):
                act.wait_ge(misc_ready, job + 1)

            def prep_ctx(b, par, groups):
                for g in groups:
                    c, n = CHUNKS[g]
                    misc_job(prep_jobs(b, "ctx")[0] + g)
                    s_.copy(ctxT[par][0:C, c:c + n], misc[0:C, 0:n]).then_inc(misc_out, 1)

            def prep_queries(b, par):
                job = prep_jobs(b, "x")[0]
                misc_job(job)
                s_.copy(xT[:, :], misc[:, 0:S]).then_inc(misc_out, 1)
                for g in range(2):
                    misc_job(job + 1 + g)
                    s_.copy(qT[par][0:C, 2 * g:2 * g + 2, :].rearrange("p h q -> p (h q)"),
                            misc[0:C, :]).then_inc(misc_out, 1)

            def prep_keys(b, groups):
                if groups[0] == 0 and not first_batch(b):
                    act.wait_ge(kparts_ready, 3 * b)
                for g in groups:
                    c, n = CHUNKS[g]
                    misc_job(prep_jobs(b, "k")[0] + g)
                    s_.activation(kf[:, c:c + n], misc[:, 0:n], ACT.Identity, bias=k.bk1[:, 0:1]).then_inc(misc_out, 1)

            def prep_values(b, groups):
                if groups[0] == 0 and not first_batch(b):
                    act.wait_ge(vs_saved, 16 * b)
                for g in groups:
                    misc_job(prep_jobs(b, "v")[0] + g)
                    n = min(4, KT - 4 * g)
                    rows_ = P if g < 3 else TAIL
                    s_.copy(vs[0:rows_, 4 * g:4 * g + n, :].rearrange("p n d -> p (n d)"),
                            misc[0:rows_, 0:n * P]).then_inc(misc_out, 1)

            def scores_out_of(s, j):
                act.wait_ge(scores_ready, j + 1)
                if not isinstance(j, int) or j >= 4:
                    act.wait_ge(pr_ready, j - 3)
                s_.copy(sc[s % 4][:, :], scores[:, 0:NK]).then_inc(scores_out, 1)

            def exp_of(b, s, j, first):
                act.wait_ge(negm_ready, j + 1)
                if not first:
                    act.wait_ge(tps_ready, TPG * (QT * (b - 1) + s // H0 + 1))
                s_.activation(pr[s][:, :], sc[s % 4][:, :], ACT.Exp, bias=negm[:, s:s + 1]).then_inc(exp_done, 1)

            def denominator(s, j):
                act.wait_ge(top_ready, j + 1)
                s_.activation(etop[:, s % 2, :], top[:, s % 4, :], ACT.Exp, bias=negm[:, s:s + 1],
                              accum_out=den[:, s:s + 1]).then_inc(den_done, 1)

            def probs_out(tile, groups):
                if groups[0] == 0 and not (isinstance(tile, int) and tile == 0):
                    act.wait_ge(ups_ready, tile)
                for g in groups:
                    act.wait_ge(tps_ready, TPG * tile + g + 1)
                    n = min(4, KT - 4 * g)
                    rows_ = P if g < 3 else TAIL
                    s_.copy(prT[0:rows_, 4 * g:4 * g + n, :].rearrange("p n q -> p (n q)"),
                            tps[g % 2][0:rows_, 0:n * P]).then_inc(tps_out, 1)

            def context_out(tile):
                act.wait_ge(ups_ready, tile + 1)
                if not (isinstance(tile, int) and tile == 0):
                    act.wait_ge(film_used, tile)
                s_.copy(uT[0:C, :], ups[0:C, 0:P]).then_inc(ups_out, 1)

            def film(tile, job):
                misc_job(job)
                if not (isinstance(tile, int) and tile == 0):
                    act.wait_ge(film_saved, 16 * tile)
                s_.copy(fs[:, :], misc[:, :]).then_inc(misc_out, 1)

            prep_ctx(0, 0, range(4))
            prep_queries(0, 0)
            scores_out_of(0, 0)
            scores_out_of(1, 1)

            def step(b, par, visit, first, last):
                for s in range(NS):
                    j = NS * b + s
                    if not (first and s < 2):
                        denominator((s - 2) % NS, j - 2)
                    exp_of(b, s, j, first)
                    if not (last and s >= NS - 2):
                        scores_out_of(s + 2, j + 2)
                    if s in GROUPS and not first:
                        probs_out(QT * b - 1, GROUPS[s])
                    if s == 3 and not first:
                        context_out(QT * b - 1)
                    if s - H0 in GROUPS:
                        probs_out(QT * b, GROUPS[s - H0])
                    if s == 7:
                        context_out(QT * b)
                    if s in (0, 4) and not first:
                        film(QT * b - (QT if s == 0 else 1), film_job(s // H0, b, last))
                    if s in (1, 2):
                        prep_keys(b, HALVES[s - 1])
                    if s == 0 and not last:
                        prep_queries(b + 1, 1 - par)
                    if s in (6, 7):
                        prep_values(b, HALVES[s - 6])
                    if s in (4, 5) and not last:
                        prep_ctx(b + 1, 1 - par, HALVES[s - 4])

            walk(act, step)
            for s in (NS - 2, NS - 1):
                denominator(s, NS * (B - 1) + s)
            for n in range(QT):
                if n:
                    probs_out(T - 1, range(TPG))
                    context_out(T - 1)
                film(T - QT + n, LAST_FILMS + n)

        @block.vector
        def _(dve):
            v = nc.vector
            st = Steps(dve, dve_step)

            def weight(b, s, j):
                dve.wait_ge(den_done, j + 1)
                st.link(v.reciprocal(rden[:, s:s + 1], den[:, s:s + 1]))
                st.link(v.tensor_tensor(rden[:, s:s + 1], rden[:, s:s + 1],
                                        k.tmask[:, bass.ds(QT * b + s // H0, 1)], ALU.mult))
                dve.sem_inc(rden_ready, 1)

            def select_all(s):
                every = Steps(dve, general_step)
                x, tp = sc[s % 4][:, :], top[:, s % 4, :]
                for r in range(TOPK // 8):
                    every.link(v.max(tp[:, 8 * r:8 * r + 8], x))
                    every.link(v.match_replace(x, tp[:, 8 * r:8 * r + 8], x, GONE))
                every.link(v.scalar_tensor_tensor(out=pr[s][:, :], in0=x, scalar=-2e38, in1=pr[s][:, :],
                                                  op0=ALU.is_le, op1=ALU.mult))
                every.restart()

            def settle(s, j):
                dve.wait_ge(doubts_ready, j + 1)
                dve.sem_inc(slot_begun, 1)
                st.link(v.tensor_copy(doubts[:, :], dps[0:1, 0:1]))
                n = dve.value_load(doubts[0:1, 0:1], min_val=0, max_val=P)
                with dve.If(n > 0):
                    select_all(s)
                dve.sem_inc(top_ready, 1)
                dve.sem_inc(pr_ready, 1)

            def pieces_of(s):
                for n, (c, w) in enumerate(PIECES):
                    st.add(v.max(cand[s % 2][:, n, :], sc[s % 4][:, c:c + w]))
                    yield

            def step(b, par, visit, first, last):
                if first:
                    dve.wait_ge(scores_out, 1)
                    for _ in pieces_of(0):
                        pass
                    st.after()
                for s in range(NS):
                    j = NS * b + s
                    if last and s == NS - 1:
                        ahead = iter(())
                    else:
                        dve.wait_ge(scores_out, j + 2)
                        dve.sem_inc(slot_begun, 1)
                        ahead = pieces_of(s + 1)

                    def link(ins):
                        st.add(ins)
                        done = st.n
                        for _ in range(2):
                            next(ahead, None)
                        dve.wait_ge(dve_step, done)

                    tp = top[:, s % 4, :]
                    x, y = (t[:, :, :].rearrange("p n e -> p (n e)") for t in (cand[s % 2], cleft))
                    for r in range(TOPK // 8):
                        link(v.max(tp[:, 8 * r:8 * r + 8], x))
                        if r == 0:
                            link(v.tensor_scalar(negm[:, s:s + 1], tp[:, 0:1], -1.0, None, ALU.mult))
                            dve.sem_inc(negm_ready, 1)
                            if not (first and s < 2):
                                weight(b if s >= 2 else b - 1, (s - 2) % NS, j - 2)
                        link(v.match_replace(y, tp[:, 8 * r:8 * r + 8], x, GONE))
                        x = y
                    st.add(v.tensor_reduce(rest[:, 0:1], cand[s % 2][:, :, 7], AX.X, ALU.max))
                    link(v.tensor_reduce(rest[:, 1:2], y, AX.X, ALU.max))
                    d = doubt[:, s % 2:s % 2 + 1]
                    link(v.tensor_reduce(d, rest[:, :], AX.X, ALU.max))
                    link(v.tensor_scalar(d, d, tp[:, TOPK - 1:TOPK], None, ALU.is_ge))
                    dve.sem_inc(doubt_ready, 1)
                    for _ in ahead:
                        pass
                    if not (first and s == 0):
                        settle((s - 1) % NS, j - 1)
                    dve.wait_ge(exp_done, j + 1)
                    dve.sem_inc(slot_begun, 1)
                    st.link(v.scalar_tensor_tensor(out=pr[s][:, :], in0=sc[s % 4][:, :], scalar=tp[:, TOPK - 1:TOPK],
                                                   in1=pr[s][:, :], op0=ALU.is_ge, op1=ALU.mult))
                st.restart()

            walk(dve, step)
            settle(NS - 1, NS * B - 1)
            for s in (NS - 2, NS - 1):
                weight(B - 1, s, NS * (B - 1) + s)


def conv_phase(nc, a, k):
    CH = 16
    with ExitStack() as ctx:
        toep = [ctx.enter_context(nc.sbuf_tensor(f"toep{i}", [P, CH, L], F32)) for i in range(2)]
        xc = [ctx.enter_context(nc.sbuf_tensor(f"xc{i}", [P, QT, CH, B], F32)) for i in range(2)]
        cv = [ctx.enter_context(nc.psum_tensor(f"cv{i}", [P, QT * CH * B], F32)) for i in range(2)]
        toep_in = [ctx.enter_context(nc.semaphore(f"toep_in{i}")) for i in range(2)]
        xc_ready, conv_done, conv_out, film_in, pool_passed = (
            ctx.enter_context(nc.semaphore(n)) for n in ("xc_ready", "conv_done", "conv_out", "film_in", "xc_passed"))
        XF, Y = k.XF, k.Y
        taps = bass.AP(k.kernpad.tensor, 1, [[1, P], [3 * P, D], [1, L]])
        flip = ctx.enter_context(nc.sbuf_tensor("flip", [P, P], F32))
        flip_ready, flipped, flip_out, flip_step = (ctx.enter_context(nc.semaphore(n)) for n in
                                                    ("flip_ready", "flipped", "flip_out", "flip_step"))
        block = ctx.enter_context(nc.Block())

        def walk(eng, step):
            for par in range(2):
                step(par, par, 0, True)
            with eng.Fori(1, D // CH // 2) as i:
                for par in range(2):
                    step(2 * i + par, par, i, False)

        def by_channel(t, c):
            return t[:, :, bass.ds(c * CH, CH)].rearrange("p (b h) d -> p h d b", h=QT)

        @block.sync
        def _(sp):
            def step(c, par, i, first):
                if not first:
                    sp.wait_ge(conv_done, c - 1)
                sp.dma_start(toep[par][:, :, :], taps[:, bass.ds(c * CH, CH), :]).then_inc(toep_in[par], 16)
            walk(sp, step)
            sp.dma_start(k.FO[:, :, :], k.film_out.rearrange("t p d -> p t d")).then_inc(film_in, 16)
            sp.wait_ge(film_in, 16)

        @block.gpsimd
        def _(pool):
            st = Steps(pool, flip_step)
            st.link(nc.gpsimd.memset(flip[:, :], 0.0))
            st.link(nc.gpsimd.affine_select(out=flip[:, :], in_=flip[:, :], compare_op=ALU.not_equal, fill=1.0,
                                            base=1 - P, pattern=[[1, P]], channel_multiplier=1))
            pool.sem_inc(flip_ready, 1)
            pool.wait_ge(flip_out, NG)

            def step(c, par, i, first):
                if not first:
                    pool.wait_ge(conv_done, c - 1)
                pool.sem_inc(pool_passed, 1)
                nc.gpsimd.tensor_copy(xc[par][:, :, :, :], by_channel(XF, c)).then_inc(xc_ready, 1)
            walk(pool, step)

        @block.tensor
        def _(pe):
            pe.wait_ge(flip_ready, 1)
            for g in range(NG):
                if g >= 2:
                    pe.wait_ge(flip_out, g - 1)
                nc.tensor.matmul(cv[g % 2][:, :], flip[:, :], group(XF, g).rearrange("p j d -> p (j d)"),
                                 start=True, stop=True).then_inc(flipped, 1)

            def step(c, par, i, first):
                pe.wait_ge(toep_in[par], 16 * (i + 1))
                pe.wait_ge(xc_ready, c + 1)
                if not first:
                    pe.wait_ge(conv_out, c - 1)
                for d in range(CH):
                    x, near, far = xc[par], toep[par][:, d, 0:P], toep[par][:, d, P:L]
                    o = [cv[par][:, (h * CH + d) * B:(h * CH + d + 1) * B] for h in range(QT)]
                    nc.tensor.matmul(o[0], near, x[:, 0, d, :], start=True, stop=True)
                    nc.tensor.matmul(o[1], near, x[:, 1, d, :], start=True, stop=False)
                    ins = nc.tensor.matmul(o[1], far, x[:, 0, d, :], start=False, stop=True)
                ins.then_inc(conv_done, 1)
            walk(pe, step)

        @block.scalar
        def _(act):
            for g in range(NG):
                act.wait_ge(flipped, g + 1)
                nc.scalar.copy(group(XF, g).rearrange("p j d -> p (j d)"), cv[g % 2][:, :]).then_inc(flip_out, 1)

            def step(c, par, i, first):
                act.wait_ge(conv_done, c + 1)
                nc.scalar.copy(by_channel(Y, c), cv[par][:, :].rearrange("p (h d b) -> p h d b", h=QT, d=CH)
                               ).then_inc(conv_out, 1)
            walk(act, step)


class GroupNorm:

    def __init__(self, nc, ctx, name):
        self.nc = nc
        self.stats = ctx.enter_context(nc.sbuf_tensor(name + "_stats", [P, GT, 6], F32))
        self.mv = ctx.enter_context(nc.sbuf_tensor(name + "_mv", [P, GT, 2], F32))
        self.var = ctx.enter_context(nc.sbuf_tensor(name + "_var", [P, GT], F32))
        self.rstd = ctx.enter_context(nc.sbuf_tensor(name + "_rstd", [P, GT], F32))
        self.var_ready = ctx.enter_context(nc.semaphore(name + "_var_ready"))
        self.rstd_ready = ctx.enter_context(nc.semaphore(name + "_rstd_ready"))

    def on_vector(self, dve, st, src, dst, n):
        v = self.nc.vector
        for j in range(GT):
            st.add(v.bn_stats(self.stats[:, j, :], src[:, j, :]))
        st.after()
        for j in range(GT):
            st.add(v.bn_aggr(self.mv[:, j, :], self.stats[:, j, :]))
        st.after()
        st.link(v.tensor_scalar(self.var[:, :], self.mv[:, :, 1], EPS, None, ALU.add))
        dve.sem_inc(self.var_ready, 1)
        dve.wait_ge(self.rstd_ready, n + 1)
        for j in range(GT):
            st.add(v.tensor_scalar(dst[:, j, :], src[:, j, :], self.mv[:, j, 0:1], self.rstd[:, j:j + 1],
                                   ALU.subtract, ALU.mult))
        st.after()

    def on_gpsimd(self, pool, mhalf, n):
        pool.wait_ge(self.var_ready, n + 1)
        self.nc.gpsimd.tensor_tensor(self.rstd[:, :], self.var[:, :], mhalf[:, 0:GT], ALU.pow
                                     ).then_inc(self.rstd_ready, 1)


def walk_groups(eng, step):
    for par in range(2):
        step(par, par, True)
    with eng.Fori(1, NG // 2) as i:
        for par in range(2):
            step(2 * i + par, par, False)


def group(t, g):
    return t[:, bass.ds(g * GT, GT), :]


def ffn0_phase(nc, a, k):
    with ExitStack() as ctx:
        def sb(name, shape, dt=F32):
            return ctx.enter_context(nc.sbuf_tensor(name, shape, dt))

        def sem(name):
            return ctx.enter_context(nc.semaphore(name))

        xt = [sb(f"xt{i}", [P, GT, D]) for i in range(2)]
        hn = [sb(f"hn{i}", [P, GT, D]) for i in range(2)]
        on = sb("on", [P, GT, D])
        hT = sb("hT", [P, GT * P])
        gl = [sb(f"gl{i}", [P, GT * P]) for i in range(4)]
        rowsb = {n: sb("r_" + n, [P, D]) for n in ("g_ffn", "b_ffn", "g_norm_out", "b_norm_out")}
        tp = ctx.enter_context(nc.psum_tensor("f_tp", [P, 512], F32))
        hp = [ctx.enter_context(nc.psum_tensor(f"f_hp{i}", [P, 512], F32)) for i in range(2)]
        op = [ctx.enter_context(nc.psum_tensor(f"f_op{i}", [P, GT, D], F32)) for i in range(2)]
        X, X0, Y, FO, ident = k.X, k.X0, k.Y, k.FO, k.ident
        n_in, n_out = GroupNorm(nc, ctx, "n_in"), GroupNorm(nc, ctx, "n_out")
        rows_in, hn_ready, tp_ready, hT_ready = sem("rows_in"), sem("hn_ready"), sem("tp_ready"), sem("hT_ready")
        hid_ready, gelu_done, out_ready, out_read, dve_step = (sem("hid_ready"), sem("gelu_done"), sem("out_ready"),
                                                               sem("out_read"), sem("dve_step_f"))
        block = ctx.enter_context(nc.Block())

        @block.sync
        def _(sp):
            for name, t in rowsb.items():
                sp.dma_start(t[:, :], a["L0_xattn_" + name].partition_broadcast(P)).then_inc(rows_in, 16)

        @block.gpsimd
        def _(pool):
            def step(g, par, first):
                n_in.on_gpsimd(pool, k.mhalf, g)
                if not (first and par == 0):
                    n_out.on_gpsimd(pool, k.mhalf, g - 1)
            walk_groups(pool, step)
            n_out.on_gpsimd(pool, k.mhalf, NG - 1)

        @block.vector
        def _(dve):
            v = nc.vector
            st = Steps(dve, dve_step)
            dve.wait_ge(rows_in, 16 * 4)
            for n in ("g_norm_out", "b_norm_out"):
                st.add(v.tensor_scalar(rowsb[n][:, :], rowsb[n][:, :], k.TG[:, 0:1], None, ALU.mult))

            def begin(g, par):
                x, f = xt[par], group(FO, g)
                st.link(v.tensor_tensor(x[:, :, :], group(Y, g), f[:, :, 0:D], ALU.mult))
                st.link(v.tensor_tensor(x[:, :, :], x[:, :, :], f[:, :, D:2 * D], ALU.add))
                st.link(v.tensor_tensor(x[:, :, :], x[:, :, :], group(X0, g), ALU.add))
                n_in.on_vector(dve, st, x, hn[par], g)
                st.link(v.tensor_tensor(hn[par][:, :, :], hn[par][:, :, :], rows(rowsb["g_ffn"][:, :], GT), ALU.mult))
                st.link(v.tensor_tensor(hn[par][:, :, :], hn[par][:, :, :], rows(rowsb["b_ffn"][:, :], GT), ALU.add))
                dve.sem_inc(hn_ready, 1)

            def finish(g, par):
                x = xt[par]
                dve.wait_ge(out_ready, g + 1)
                st.link(v.tensor_tensor(x[:, :, :], op[par][:, :, :], x[:, :, :], ALU.add))
                dve.sem_inc(out_read, 1)
                n_out.on_vector(dve, st, x, on, g)
                st.link(v.tensor_tensor(on[:, :, :], on[:, :, :], rows(rowsb["g_norm_out"][:, :], GT), ALU.mult))
                st.link(v.tensor_tensor(on[:, :, :], on[:, :, :], rows(rowsb["b_norm_out"][:, :], GT), ALU.add))
                st.link(v.tensor_tensor(group(X, g), group(X, g), on[:, :, :], ALU.add))

            def step(g, par, first):
                begin(g, par)
                if not (first and par == 0):
                    finish(g - 1, 1 - par)
                st.restart()

            walk_groups(dve, step)
            finish(NG - 1, 1)

        @block.tensor
        def _(pe):
            t = nc.tensor

            def step(g, par, first):
                pe.wait_ge(hn_ready, g + 1)
                for j in range(GT):
                    ins = t.transpose(tp[:, j * P:j * P + P], hn[par][:, j, :], ident[:, :])
                ins.then_inc(tp_ready, 1)
                pe.wait_ge(hT_ready, g + 1)
                for c in range(4):
                    if not (first and par == 0 and c < 2):
                        pe.wait_ge(gelu_done, 4 * g + c - 1)
                    t.matmul(hp[c % 2][:, :], k.w1_0[:, c * P:c * P + P], hT[:, :], start=True, stop=True
                             ).then_inc(hid_ready, 1)
                if not first:
                    pe.wait_ge(out_read, g - 1)
                pe.wait_ge(gelu_done, 4 * g + 4)
                for j in range(GT):
                    for c in range(4):
                        t.matmul(op[par][:, j, :], gl[c][:, j * P:j * P + P], k.w2_0[:, c, :], start=(c == 0), stop=False)
                    ins = t.matmul(op[par][:, j, :], k.ones[0:1, :], k.b2_0[0:1, :], start=False, stop=True)
                ins.then_inc(out_ready, 1)

            walk_groups(pe, step)

        @block.scalar
        def _(act):
            def step(g, par, first):
                act.wait_ge(tp_ready, g + 1)
                nc.scalar.copy(hT[:, :], tp[:, :]).then_inc(hT_ready, 1)
                if not (first and par == 0):
                    act.wait_ge(out_ready, g)
                for c in range(4):
                    act.wait_ge(hid_ready, 4 * g + c + 1)
                    nc.scalar.activation(gl[c][:, :], hp[c % 2][:, :], ACT.Gelu, bias=k.b1_0[:, c:c + 1]
                                         ).then_inc(gelu_done, 1)
            walk_groups(act, step)


def mixture0_phase(nc, a, k):
    with ExitStack() as ctx:
        def sb(name, shape, dt=F32):
            return ctx.enter_context(nc.sbuf_tensor(name, shape, dt))

        def sem(name):
            return ctx.enter_context(nc.semaphore(name))

        def ps(name, shape):
            return ctx.enter_context(nc.psum_tensor(name, shape, F32))

        xg = [sb(f"m_xg{i}", [P, GT, D]) for i in range(2)]
        hn = [sb(f"m_hn{i}", [P, GT, D]) for i in range(2)]
        hT = [sb(f"m_hT{i}", [P, GT * P]) for i in range(2)]
        lo, ex = sb("m_lo", [P, GT, E]), sb("m_ex", [P, GT, E])
        mx, sm, gate = sb("m_mx", [P, GT]), sb("m_sm", [P, GT]), sb("m_gate", [P, GT])
        pri, keep = sb("m_pri", [P, GT, E]), sb("m_keep", [P, GT, E])
        rank = sb("m_rank", [P, E])
        oh = [sb(f"m_oh{i}", [P, GT, E], BF16) for i in range(2)]
        prior = [sb(f"m_prior{i}", [P, GT + 1, E], BF16) for i in range(2)]
        wt = [sb(f"m_wt{i}", [P, GT, E]) for i in range(2)]
        wtT = sb("m_wtT", [E, GT * P])
        before, all1 = sb("m_before", [P, P], BF16), sb("m_all1", [P, P], BF16)
        tp, small = ps("m_tp", [P, 512]), ps("m_small", [P, 512])
        wp, bp = ps("m_wp", [P, 512]), ps("m_bp", [P, GT, D])
        ep = [ps(f"m_ep{i}", [P, 4, D]) for i in range(4)]
        X, ident = k.X, k.ident
        n_m = GroupNorm(nc, ctx, "n_m")
        consts, hn_ready, tp_ready, hT_ready, logits_ready = (sem("m_consts"), sem("m_hn_ready"), sem("m_tp_ready"),
                                                              sem("m_hT_ready"), sem("m_logits_ready"))
        centred, exp_done, oh_ready, loc_ready, wt_ready, wp_ready, wtT_ready, bias_ready = (
            sem("m_centred"), sem("m_exp_done"), sem("m_oh_ready"), sem("m_loc_ready"), sem("m_wt_ready"),
            sem("m_wp_ready"), sem("m_wtT_ready"), sem("m_bias_ready"))
        exp_ready, exp_read, group_done, dve_step = (sem("m_experts_ready"), sem("m_experts_read"), sem("m_group_done"),
                                                     sem("m_dve_step"))
        pool_step = sem("m_pool_step")
        block = ctx.enter_context(nc.Block())

        @block.gpsimd
        def _(pool):
            g_ = nc.gpsimd
            st = Steps(pool, pool_step)
            st.link(g_.memset(all1[:, :], 1.0))
            st.link(g_.affine_select(out=before[:, :], in_=all1[:, :], compare_op=ALU.is_gt, fill=0.0, base=0,
                                     pattern=[[1, P]], channel_multiplier=-1))
            st.link(g_.iota(rank[:, :], [[-1, E]], base=E, channel_multiplier=0, allow_small_or_imprecise_dtypes=True))
            st.link(g_.memset(prior[1][:, GT, :], 0.0))
            pool.sem_inc(consts, 1)
            walk_groups(pool, lambda g, par, first: n_m.on_gpsimd(pool, k.mhalf, g))

        @block.vector
        def _(dve):
            v = nc.vector
            st = Steps(dve, dve_step)
            dve.wait_ge(consts, 1)

            def route(g, par):
                st.link(v.tensor_copy(xg[par][:, :, :], group(X, g)))
                n_m.on_vector(dve, st, xg[par], hn[par], g)
                dve.sem_inc(hn_ready, 1)
                dve.wait_ge(logits_ready, g + 1)
                lg = small[:, 0:GT * E].rearrange("p (j e) -> p j e", e=E)
                st.link(v.tensor_reduce(mx[:, :], lg, AX.X, ALU.max))
                st.link(v.tensor_tensor(lo[:, :, :], lg, over(mx[:, :], E), ALU.subtract))
                dve.sem_inc(centred, 1)
                st.link(v.tensor_scalar(pri[:, :, :], lo[:, :, :], 0.0, None, ALU.is_equal))
                st.link(v.tensor_tensor(pri[:, :, :], pri[:, :, :], rows(rank[:, :], GT), ALU.mult))
                st.link(v.tensor_reduce(mx[:, :], pri[:, :, :], AX.X, ALU.max))
                st.link(v.tensor_tensor(oh[par][:, :, :], pri[:, :, :], over(mx[:, :], E), ALU.is_equal))
                st.link(v.tensor_copy(prior[par][:, 0, :], prior[1 - par][:, GT, :]))
                for j in range(GT):
                    st.link(v.tensor_tensor(prior[par][:, j + 1, :], prior[par][:, j, :], oh[par][:, j, :], ALU.add))
                dve.sem_inc(oh_ready, 1)
                dve.wait_ge(exp_done, g + 1)
                st.link(v.tensor_reduce(sm[:, :], ex[:, :, :], AX.X, ALU.add))
                st.link(v.reciprocal(gate[:, :], sm[:, :]))
                st.link(v.tensor_scalar(gate[:, :], gate[:, :], k.TG[:, 2:3], None, ALU.mult))
                dve.wait_ge(loc_ready, g + 1)
                place = small[:, 64:64 + GT * E].rearrange("p (j e) -> p j e", e=E)
                st.link(v.tensor_scalar(keep[:, :, :], place, float(CAP), None, ALU.is_lt))
                st.link(v.tensor_tensor(keep[:, :, :], keep[:, :, :], oh[par][:, :, :], ALU.mult))
                st.link(v.tensor_tensor(wt[par][:, :, :], keep[:, :, :], over(gate[:, :], E), ALU.mult))
                dve.sem_inc(wt_ready, 1)

            def combine(g, par):
                for j in range(GT):
                    for half in range(2):
                        job = 2 * (GT * g + j) + half
                        dve.wait_ge(exp_ready, job + 1)
                        for e in range(4):
                            x = xg[par][:, j, :]
                            st.link(v.scalar_tensor_tensor(out=x, in0=ep[(2 * j + half) % 4][:, e, :],
                                                           scalar=wt[par][:, j, 4 * half + e:4 * half + e + 1], in1=x,
                                                           op0=ALU.mult, op1=ALU.add))
                        dve.sem_inc(exp_read, 1)
                dve.wait_ge(bias_ready, g + 1)
                st.link(v.tensor_tensor(group(X, g), bp[:, :, :], xg[par][:, :, :], ALU.add))
                dve.sem_inc(group_done, 1)

            def step(g, par, first):
                route(g, par)
                if not (first and par == 0):
                    combine(g - 1, 1 - par)
                st.restart()

            walk_groups(dve, step)
            combine(NG - 1, 1)

        @block.tensor
        def _(pe):
            t = nc.tensor

            def experts(g, par, started):
                for j in range(GT):
                    for half in range(2):
                        slot = (2 * j + half) % 4
                        if started or 2 * j + half >= 4:
                            pe.wait_ge(exp_read, 2 * (GT * g + j) + half - 3)
                        t.matmul(ep[slot][:, :, :], hT[par][:, j * P:j * P + P], k.wm0[:, 4 * half:4 * half + 4, :],
                                 start=True, stop=True).then_inc(exp_ready, 1)

            def bias(g, par, started):
                pe.wait_ge(wt_ready, g + 1)
                for j in range(GT):
                    ins = t.transpose(wp[0:E, j * P:j * P + P], wt[par][:, j, :], ident[:, :])
                ins.then_inc(wp_ready, 1)
                pe.wait_ge(wtT_ready, g + 1)
                if started:
                    pe.wait_ge(group_done, g)
                for j in range(GT):
                    ins = t.matmul(bp[:, j, :], wtT[:, j * P:j * P + P], k.bm0[:, :], start=True, stop=True)
                ins.then_inc(bias_ready, 1)

            def step(g, par, first):
                pe.wait_ge(hn_ready, g + 1)
                for j in range(GT):
                    ins = t.transpose(tp[:, j * P:j * P + P], hn[par][:, j, :], ident[:, :])
                ins.then_inc(tp_ready, 1)
                pe.wait_ge(hT_ready, g + 1)
                for j in range(GT):
                    ins = t.matmul(small[:, j * E:j * E + E], hT[par][:, j * P:j * P + P], k.wg0[:, :],
                                   start=True, stop=True)
                ins.then_inc(logits_ready, 1)
                pe.wait_ge(oh_ready, g + 1)
                for j in range(GT):
                    o = small[:, 64 + j * E:64 + j * E + E]
                    t.matmul(o, before[:, :], oh[par][:, j, :], start=True, stop=False)
                    ins = t.matmul(o, all1[:, :], prior[par][:, j, :], start=False, stop=True)
                ins.then_inc(loc_ready, 1)
                if not (first and par == 0):
                    bias(g - 1, 1 - par, not (first and par == 1))
                    experts(g - 1, 1 - par, not (first and par == 1))

            walk_groups(pe, step)
            bias(NG - 1, 1, True)
            experts(NG - 1, 1, True)

        @block.scalar
        def _(act):
            def bias(g):
                act.wait_ge(wp_ready, g + 1)
                nc.scalar.copy(wtT[:, :], wp[0:E, :]).then_inc(wtT_ready, 1)

            def step(g, par, first):
                act.wait_ge(tp_ready, g + 1)
                if not first:
                    act.wait_ge(group_done, g - 1)
                nc.scalar.copy(hT[par][:, :], tp[:, :]).then_inc(hT_ready, 1)
                act.wait_ge(centred, g + 1)
                nc.scalar.activation(ex[:, :, :], lo[:, :, :], ACT.Exp).then_inc(exp_done, 1)
                if not (first and par == 0):
                    bias(g - 1)

            walk_groups(act, step)
            bias(NG - 1)


def queries_phase(nc, a, k):
    with ExitStack() as ctx:
        def sb(name, shape, dt=F32):
            return ctx.enter_context(nc.sbuf_tensor(name, shape, dt))

        def sem(name):
            return ctx.enter_context(nc.semaphore(name))

        hn = [sb(f"q_hn{i}", [P, GT, D]) for i in range(2)]
        hT = [sb(f"q_hT{i}", [P, GT * P]) for i in range(2)]
        qf = [sb(f"q_f{i}", [P, GT * P]) for i in range(2)]
        parts = [[sb(f"q_p{i}{n}", [P, GT * P], BF16) for n in range(3)] for i in range(2)]
        tp = [ctx.enter_context(nc.psum_tensor(f"q_tp{i}", [P, 512], F32)) for i in range(2)]
        qp = [ctx.enter_context(nc.psum_tensor(f"q_qp{i}", [P, 512], F32)) for i in range(2)]
        X, ident = k.X, k.ident
        n_q = GroupNorm(nc, ctx, "n_q")
        hn_ready, tp_ready, hT_ready, qp_ready, qf_ready = (sem("q_hn_ready"), sem("q_tp_ready"), sem("q_hT_ready"),
                                                            sem("q_qp_ready"), sem("q_qf_ready"))
        parts_ready, dve_step = sem("q_parts_ready"), sem("q_dve_step")
        saved = [sem(f"q_saved{i}") for i in range(2)]
        block = ctx.enter_context(nc.Block())

        @block.gpsimd
        def _(pool):
            walk_groups(pool, lambda g, par, first: n_q.on_gpsimd(pool, k.mhalf, g))

        @block.vector
        def _(dve):
            v = nc.vector
            st = Steps(dve, dve_step)

            def split(g, par):
                dve.wait_ge(qf_ready, g + 1)
                for n in range(3):
                    st.link(v.tensor_copy(parts[par][n][:, :], qf[par][:, :]))
                    if n < 2:
                        st.link(v.tensor_tensor(qf[par][:, :], qf[par][:, :], parts[par][n][:, :], ALU.subtract))
                dve.sem_inc(parts_ready, 1)

            def step(g, par, i):
                if not isinstance(i, int):
                    dve.wait_ge(saved[par], 48 * i)
                n_q.on_vector(dve, st, group(X, g), hn[par], g)
                dve.sem_inc(hn_ready, 1)
                split(g, par)
                st.restart()

            for par in range(2):
                step(par, par, 0)
            with dve.Fori(1, NG // 2) as i:
                for par in range(2):
                    step(2 * i + par, par, i)

        @block.tensor
        def _(pe):
            def step(g, par, first):
                pe.wait_ge(hn_ready, g + 1)
                for j in range(GT):
                    ins = nc.tensor.transpose(tp[par][:, j * P:j * P + P], hn[par][:, j, :], ident[:, :])
                ins.then_inc(tp_ready, 1)
                pe.wait_ge(hT_ready, g + 1)
                nc.tensor.matmul(qp[par][:, :], k.wq1[:, :], hT[par][:, :], start=True, stop=True).then_inc(qp_ready, 1)
            walk_groups(pe, step)

        @block.scalar
        def _(act):
            def step(g, par, first):
                act.wait_ge(tp_ready, g + 1)
                nc.scalar.copy(hT[par][:, :], tp[par][:, :]).then_inc(hT_ready, 1)
                act.wait_ge(qp_ready, g + 1)
                nc.scalar.activation(qf[par][:, :], qp[par][:, :], ACT.Identity, bias=k.bq1[:, 0:1],
                                     scale=DH1 ** -0.5).then_inc(qf_ready, 1)
            walk_groups(act, step)

        @block.sync
        def _(sp):
            def step(g, par, first):
                sp.wait_ge(parts_ready, g + 1)
                for n in range(3):
                    sp.dma_start(k.queries[n, :, bass.ds(g * GT * P, GT * P)], parts[par][n][:, :]
                                 ).then_inc(saved[par], 16)
            walk_groups(sp, step)
            for par in range(2):
                sp.wait_ge(saved[par], 48 * NG // 2)


def attention1_phase(nc, a, k):
    PAIRS = [(0, 0), (1, 0), (2, 0), (0, 1), (1, 1), (2, 1), (0, 2)]
    ROWS = 64
    GUARD = DH1 * len(PAIRS)
    HG = H1 // 4
    VW = 32
    UNITS = 2 * KT
    MJ = 4 * QT * 2
    with ExitStack() as ctx:
        def sb(name, shape, dt=F32):
            return ctx.enter_context(nc.sbuf_tensor(name, shape, dt))

        def sem(name):
            return ctx.enter_context(nc.semaphore(name))

        ks = [sb(f"ks{i}", [P, H1 // 2, NK], BF16) for i in range(2)]
        qs = [sb(f"qs{i}", [P, H1, S], BF16) for i in range(2)]
        vn = sb("vn", [P, KT, D])
        va = [sb(f"va{i}", [P, KT, H1, VW]) for i in range(2)]
        pb = [sb(f"pb{i}", [P, 2, S]) for i in range(8)]
        mx2 = sb("mx2", [P, QT, H1, 2])
        mneg = sb("mneg", [P, QT, H1])
        mparts = sb("mparts", [P, QT, 3, 2, H1 // 2], BF16)
        identb = sb("identb", [P, P], BF16)
        mT = sb("mT", [3 * H1, QT, P], BF16)
        ot = [sb(f"ot{i}", [P, S]) for i in range(2)]
        rd = sb("rd", [P, QT, 4])
        ao = sb("ao", [P, QT, D])
        aoT = sb("aoT", [P, S])
        wps = [ctx.enter_context(nc.psum_tensor(f"wps{i}", [P, 1024], F32)) for i in range(2)]
        sps = [ctx.enter_context(nc.psum_tensor(f"sps{i}", [P, 2, S], F32)) for i in range(2)]
        ops = [ctx.enter_context(nc.psum_tensor(f"ops{i}", [P, 512], F32)) for i in range(2)]
        X, ident = k.X, k.ident

        ready, vn_in, va_ready = sem("a_ready"), sem("vn_in"), sem("va_ready")
        kq_in = [[sem(f"kq_in{i}{g}") for g in range(HG)] for i in range(2)]
        work_ready, work_read = sem("work_ready"), sem("work_read")
        mparts_ready, mT_ready, mT_saved, guard_in = (sem("mparts_ready"), sem("mT_ready"), sem("mT_saved"),
                                                      sem("guard_in"))
        s_ready, p_ready, pv_done, ops_read = sem("s_ready"), sem("p_ready"), sem("pv_done"), sem("ops_read")
        pe_passed, pool_passed, ks_ready = sem("a_pe_passed"), sem("a_pool_passed"), sem("ks_ready")
        ao_ready, aoT_ready, dve_step, pool_step = sem("ao_ready"), sem("aoT_ready"), sem("a_dve_step"), sem("a_pool_step")
        block = ctx.enter_context(nc.Block())

        class Part:

            def nothing(*_):
                pass

            def __init__(self):
                self.maxima = self.split_maxima = self.guard = self.scores = self.values = Part.nothing
                self.group_end = self.result = self.turn = self.output = self.batch_end = Part.nothing

        START = HG * MJ + 2 + MJ
        PER = HG * MJ + 2 + HG + 2

        def base(b):
            if isinstance(b, int) and b == 0:
                return START
            return START + PER * b - 3 - (MJ if isinstance(b, int) and b == B - 1 else 0)

        def job_slot(b, n):
            return (n + (0 if isinstance(b, int) and b == 0 else 1) + START) % 2

        def walk(eng, do):
            count = [0]

            def job(part, b0, *args):
                n = count[0]
                count[0] += 1
                part(*args, base(b0) + n, wps[job_slot(b0, n)])

            def batch(b, par, visits, first, follow):
                count[0] = 0
                for g in range(HG):
                    mg = (g + 1) % HG
                    ahead = 1 if g < HG - 1 else 2
                    beside = follow >= ahead
                    if g == HG - 1 and follow >= 1:
                        do.split_maxima(b + 1)
                    for kt in range(KT):
                        for u in (2 * kt, 2 * kt + 1):
                            do.scores(b, par, g, u, first)
                        if kt:
                            do.values(b, par, g, kt - 1, first)
                        if beside:
                            for n in range(MJ * kt // KT, MJ * (kt + 1) // KT):
                                job(do.maxima, b, b + ahead, (par + ahead) % 2, visits[ahead], 4 * mg + n // 4,
                                    n // 2 % 2, n % 2)
                        if kt == 3 and g:
                            job(do.result, b, b, g - 1)
                        if kt == 3 and not g and not first:
                            job(do.result, b, b - 1, HG - 1)
                        if kt == 5 and not g and not first:
                            job(do.turn, b, b - 1)
                        if kt == 7 and not g and not first:
                            job(do.output, b, b - 1)
                        if g == HG - 1 and follow >= 1 and kt in (5, 6):
                            job(do.guard, b, b + 1, kt - 5)
                    do.values(b, par, g, KT - 1, first)
                    do.group_end(b, g, first)
                do.batch_end()

            for g in range(HG + 1):
                for n in range(MJ):
                    if g == HG and n == MJ // 2:
                        do.split_maxima(0)
                    num = g * MJ + n
                    do.maxima(g // HG, g // HG, 1, 4 * (g % HG) + n // 4, n // 2 % 2,
                                                            n % 2, num, wps[num % 2])
            for q in range(2):
                num = (HG + 1) * MJ + q
                do.guard(0, q, num, wps[num % 2])
            do.batch_end()
            batch(0, 0, {1: 1, 2: 2}, True, 2)
            with eng.Fori(0, (B - 4) // 2) as i:
                batch(2 * i + 1, 1, {1: i + 2, 2: i + 2}, False, 2)
                batch(2 * i + 2, 0, {1: i + 2, 2: i + 3}, False, 2)
            batch(B - 3, 1, {1: B // 2, 2: B // 2}, False, 2)
            batch(B - 2, 0, {1: B // 2}, False, 1)
            batch(B - 1, 1, {}, False, 0)
            end = base(B - 1) + count[0]
            for n, (part, args) in enumerate(((do.result, (B - 1, HG - 1)), (do.turn, (B - 1,)), (do.output, (B - 1,)))):
                part(*args, end + n, wps[(job_slot(B - 1, count[0]) + n) % 2])

        @block.gpsimd
        def _(pool):
            g_ = nc.gpsimd
            st = Steps(pool, pool_step)
            st.link(g_.memset(identb[:, :], 0.0))
            st.link(g_.affine_select(out=identb[:, :], in_=identb[:, :], compare_op=ALU.not_equal, fill=1.0, base=0,
                                     pattern=[[-1, P]], channel_multiplier=1))
            for i in range(2):
                st.link(g_.memset(qs[i][:, :, :], 0.0))
                pool.sem_inc(ready, 1)
            for i in range(2):
                st.add(g_.memset(va[i][:, :, :, :], 0.0))
            st.after()
            for i in range(2):
                st.add(g_.memset(va[i][:, :, :, DH1:DH1 + 1], 1.0))
            st.restart()

            def spread_values(b, par):
                pool.wait_ge(vn_in, 16 * (b + 1))
                if not isinstance(b, int):
                    pool.wait_ge(pv_done, KT * HG * (b - 1))
                pool.sem_inc(pool_passed, 1)
                for kt in range(KT):
                    st.add(g_.tensor_copy(va[par][0:kn(kt), kt, :, 0:DH1],
                                          vn[0:kn(kt), kt, :].rearrange("p (h d) -> p h d", d=DH1)))
                st.restart()
                pool.sem_inc(va_ready, 1)

            spread_values(0, 0)
            spread_values(1, 1)
            with pool.Fori(1, B // 2) as i:
                spread_values(2 * i, 0)
                spread_values(2 * i + 1, 1)

        @block.sync
        def _(sp):
            kall = k.keys.rearrange("b n (pr o d) c -> b o n d pr c", o=2, d=DH1)
            qall = k.queries.rearrange("n (pr o d) c -> o n d pr c", o=2, d=DH1)

            def load(b, par, g, started):
                if started:
                    sp.wait_ge(pv_done, KT * (HG * (b - 2) + g + 1))
                pr = slice(2 * g, 2 * g + 2)
                for odd in range(2):
                    kb = kall[bass.ds(b, 1), odd, :, :, pr, :].rearrange("b n d pr c -> (b n) d pr c")
                    qb = qall[odd, :, :, pr, bass.ds(b * S, S)]
                    for i, (qp, kp) in enumerate(PAIRS):
                        r = slice(ROWS * odd + DH1 * i, ROWS * odd + DH1 * (i + 1))
                        sp.dma_start(ks[par][r, pr, :], kb[kp]).then_inc(kq_in[par][g], 16)
                        sp.dma_start(qs[par][r, 4 * g + odd:4 * g + 4:2, :], qb[qp]).then_inc(kq_in[par][g], 16)

            def load_values(b, started):
                if started:
                    sp.wait_ge(va_ready, b)
                sp.dma_start(vn[:, :, :].rearrange("p n d -> p (n d)"),
                             k.values[bass.ds(b, 1), :, :].rearrange("o p c -> (o p) c")).then_inc(vn_in, 16)

            def guard(b, par, started):
                if started:
                    sp.wait_ge(guard_in, 32 * (b - 1))
                sp.wait_ge(mT_ready, 2 * b + 2)
                sp.dma_start(k.guards[par], mT[:, :, :].rearrange("r h p -> r (h p)")).then_inc(mT_saved, 16)
                sp.wait_ge(mT_saved, 16 * (b + 1))
                src = k.guards[par].rearrange("(n o h) c -> o n h c", n=3, o=2)
                for odd in range(2):
                    r = ROWS * odd + GUARD
                    sp.dma_start(qs[par][r:r + 3, odd:H1:2, :], src[odd]).then_inc(guard_in, 16)

            for b in range(2):
                sp.wait_ge(ready, b + 1)
                sp.wait_ge(ks_ready, b + 1)
                for g in range(HG):
                    load(b, b, g, False)
                load_values(b, b == 1)
            guard(0, 0, False)

            def batch(b, par):
                for g in range(HG - 1):
                    load(b + 2, par, g, True)
                load_values(b + 2, True)
                guard(b + 1, 1 - par, not (isinstance(b, int) and b == 0))
                load(b + 2, par, HG - 1, True)

            batch(0, 0)
            with sp.Fori(0, (B - 4) // 2) as i:
                batch(2 * i + 1, 1)
                batch(2 * i + 2, 0)
            batch(B - 3, 1)
            guard(B - 1, 1, True)
            sp.wait_ge(guard_in, 32 * B)

        @block.tensor
        def _(pe):
            t = nc.tensor
            do = Part()

            def work(job):
                if not (isinstance(job, int) and job < 2):
                    pe.wait_ge(work_read, job - 1)

            def maxima(b, par, visit, h, q, c, job, buf):
                if h % 4 == 0 and q == 0 and c == 0:
                    pe.wait_ge(kq_in[par][h // 4], 16 * 2 * 2 * len(PAIRS) * visit)
                work(job)
                lo, hi = ((0, 1024), (1024, NK))[c]
                for k0 in range(lo, hi, 512):
                    w = min(512, hi - k0)
                    ins = t.matmul(buf[:, k0 - lo:k0 - lo + w], qs[par][:, h, q * P:q * P + P],
                                   ks[par][:, h // 2, k0:k0 + w], start=True, stop=True)
                ins.then_inc(work_ready, 1)

            def guard(b, q, job, buf):
                pe.wait_ge(mparts_ready, b + 1)
                work(job)
                pe.sem_inc(pe_passed, 1)
                t.transpose(buf[0:3 * H1, 0:P // 2].bitcast(BF16), mparts[:, q, :, :, :].rearrange("p n o h -> p (n o h)"),
                            identb[:, :]).then_inc(work_ready, 1)

            def scores(b, par, g, u, first):
                if g == 0 and u == 0:
                    pe.wait_ge(guard_in, 32 * (b + 1))
                kt, pair = u // 2, u % 2
                n = UNITS * HG * b + UNITS * g + u
                if not (isinstance(n, int) and n < 2):
                    pe.wait_ge(p_ready, n - 1)
                for i in range(2):
                    h = 4 * g + 2 * pair + i
                    ins = t.matmul(sps[u % 2][0:kn(kt), i, :], ks[par][:, h // 2, kt * P:kt * P + kn(kt)],
                                   qs[par][:, h, :], start=True, stop=True)
                ins.then_inc(s_ready, 1)

            def values(b, par, g, kt, first):
                if g == 0 and kt == 0:
                    pe.wait_ge(va_ready, b + 1)
                if kt == 0 and not (first and g < 2):
                    pe.wait_ge(ops_read, HG * b + g - 1)
                pe.wait_ge(p_ready, UNITS * HG * b + UNITS * g + 2 * kt + 2)
                for i in range(4):
                    ins = t.matmul(ops[g % 2][VW * i:VW * i + VW, 0:S], va[par][0:kn(kt), kt, 4 * g + i, :],
                                   pb[(UNITS * g + 2 * kt + i // 2) % 8][0:kn(kt), i % 2, :],
                                   start=(kt == 0), stop=(kt == KT - 1))
                ins.then_inc(pv_done, 1)

            def result(b, g, job, buf):
                pe.wait_ge(ops_read, HG * b + g + 1)
                work(job)
                for q in range(QT):
                    ins = t.transpose(buf[:, q * P:q * P + P], ot[g % 2][:, q * P:q * P + P], ident[:, :])
                ins.then_inc(work_ready, 1)

            def turn(b, job, buf):
                pe.wait_ge(ao_ready, b + 1)
                work(job)
                for q in range(QT):
                    ins = t.transpose(buf[:, q * P:q * P + P], ao[:, q, :], ident[:, :])
                ins.then_inc(work_ready, 1)

            def output(b, job, buf):
                pe.wait_ge(aoT_ready, b + 1)
                work(job)
                for q in range(QT):
                    o = buf[:, q * P:q * P + P]
                    t.matmul(o, aoT[:, q * P:q * P + P], k.wo1[:, :], start=True, stop=False)
                    ins = t.matmul(o, k.ones[0:1, :], k.bo1[0:1, :], start=False, stop=True)
                ins.then_inc(work_ready, 1)

            do.maxima, do.guard, do.scores, do.values = maxima, guard, scores, values
            do.result, do.turn, do.output = result, turn, output
            walk(pe, do)

        @block.scalar
        def _(act):
            do = Part()

            def scores(b, par, g, u, first):
                n = UNITS * HG * b + UNITS * g + u
                act.wait_ge(s_ready, n + 1)
                if not (first and UNITS * g + u < 8):
                    act.wait_ge(pv_done, KT * HG * b + (UNITS * g + u) // 2 - 3)
                rows_ = kn(u // 2)
                nc.scalar.activation(pb[(UNITS * g + u) % 8][0:rows_, :, :], sps[u % 2][0:rows_, :, :], ACT.Exp
                                     ).then_inc(p_ready, 1)

            do.scores = scores
            walk(act, do)

        @block.vector
        def _(dve):
            v = nc.vector
            st = Steps(dve, dve_step)
            do = Part()
            for i in range(2):
                st.link(v.memset(ks[i][:, :, :], 1.0))
                dve.sem_inc(ks_ready, 1)

            def maxima(b, par, visit, h, q, c, job, buf):
                dve.wait_ge(work_ready, job + 1)
                w = (1024, NK - 1024)[c]
                v.tensor_reduce(mx2[:, q, h, c:c + 1], buf[:, 0:w], AX.X, ALU.max).then_inc(work_read, 1)
                maxima.last = job

            def split_maxima(b):
                dve.wait_ge(work_read, maxima.last + 1)
                st.link(v.tensor_reduce(mneg[:, :, :], mx2[:, :, :, :], AX.X, ALU.max, negate=True))
                rest = mneg[:, :, :].rearrange("p q (h o) -> p q o h", o=2)
                for n in range(3):
                    st.link(v.tensor_copy(mparts[:, :, n, :, :], rest))
                    if n < 2:
                        st.link(v.tensor_tensor(rest, rest, mparts[:, :, n, :, :], ALU.subtract))
                dve.sem_inc(mparts_ready, 1)

            def guard(b, q, job, buf):
                dve.wait_ge(work_ready, job + 1)
                if q == 0 and not (isinstance(b, int) and b == 0):
                    dve.wait_ge(mT_saved, 16 * b)
                st.link(v.tensor_copy(mT[:, q, :], buf[0:3 * H1, 0:P // 2].bitcast(BF16)))
                dve.sem_inc(work_read, 1)
                dve.sem_inc(mT_ready, 1)

            def group_end(b, g, first):
                dve.wait_ge(pv_done, KT * (HG * b + g + 1))
                v.tensor_copy(ot[g % 2][:, :], ops[g % 2][:, 0:S]).then_inc(ops_read, 1)

            def result(b, g, job, buf):
                dve.wait_ge(work_ready, job + 1)
                r = buf[:, 0:QT * P].rearrange("p (q j w) -> p q j w", q=QT, w=VW)
                st.link(v.reciprocal(rd[:, :, :], r[:, :, :, DH1]))
                o = ao[:, :, 4 * DH1 * g:4 * DH1 * (g + 1)].rearrange("p q (j d) -> p q j d", d=DH1)
                for q in range(QT):
                    st.add(v.tensor_tensor(o[:, q], r[:, q, :, 0:DH1], over(rd[:, q, :], DH1), ALU.mult))
                st.after()
                dve.sem_inc(work_read, 1)
                if g == HG - 1:
                    dve.sem_inc(ao_ready, 1)

            def turn(b, job, buf):
                dve.wait_ge(work_ready, job + 1)
                st.link(v.tensor_copy(aoT[:, :], buf[:, 0:S]))
                dve.sem_inc(work_read, 1)
                dve.sem_inc(aoT_ready, 1)

            def output(b, job, buf):
                dve.wait_ge(work_ready, job + 1)
                x = X[:, bass.ds(QT * b, QT), :].rearrange("p q d -> p (q d)")
                st.link(v.scalar_tensor_tensor(out=x, in0=buf[:, 0:QT * D], scalar=k.TG[:, 1:2], in1=x, op0=ALU.mult,
                                               op1=ALU.add))
                dve.sem_inc(work_read, 1)

            do.maxima, do.guard, do.split_maxima, do.group_end = maxima, guard, split_maxima, group_end
            do.result, do.turn, do.output = result, turn, output
            do.batch_end = st.restart
            walk(dve, do)


def mixture1_phase(nc, a, k):
    with ExitStack() as ctx:
        def sb(name, shape, dt=F32):
            return ctx.enter_context(nc.sbuf_tensor(name, shape, dt))

        def sem(name):
            return ctx.enter_context(nc.semaphore(name))

        def ps(name, shape=(P, 512)):
            return ctx.enter_context(nc.psum_tensor(name, list(shape), F32))

        w1 = sb("e_w1", [P, E, HID])
        w2 = sb("e_w2", [P, E, 4, D])
        b1, b2, wg, bg = sb("e_b1", [P, E, 4]), sb("e_b2", [E, D]), sb("e_wg", [P, E]), sb("e_bg", [1, E])
        hn = [sb(f"e_hn{i}", [P, GT, D]) for i in range(2)]
        hT = [sb(f"e_hT{i}", [P, GT * P]) for i in range(2)]
        lg, mx, oh = sb("e_lg", [P, GT, E]), sb("e_mx", [P, GT]), sb("e_oh", [P, GT, E])
        ohT = [sb(f"e_ohT{i}", [E, GT * P]) for i in range(2)]
        ohTb = [sb(f"e_ohTb{i}", [E, GT * P], BF16) for i in range(2)]
        sel = sb("e_sel", [E, E, P], BF16)
        rank = sb("e_rank", [P, E])
        mask = [sb(f"e_mask{i}", [P, GT * P]) for i in range(2)]
        hm = [sb(f"e_hm{i}", [P, GT * P]) for i in range(2)]
        hr = [sb(f"e_hr{i}", [P, GT * P]) for i in range(2)]
        yT = sb("e_yT", [P, GT * P])
        xo = sb("e_xo", [P, GT, D])
        tp, small = ps("e_tp"), ps("e_small")
        mp = ps("e_mp")
        hp = [ps(f"e_hp{i}") for i in range(2)]
        yp = ps("e_yp")
        zp = ps("e_zp")
        X, ident = k.X, k.ident
        n_e = GroupNorm(nc, ctx, "n_e")
        w_in, consts = sem("e_w_in"), sem("e_consts")
        hn_ready, tp_ready, hT_ready, lg_ready, oh_ready, ohp_ready, ohT_ready = (
            sem("e_hn_ready"), sem("e_tp_ready"), sem("e_hT_ready"), sem("e_lg_ready"), sem("e_oh_ready"),
            sem("e_ohp_ready"), sem("e_ohT_ready"))
        mp_ready, mask_ready, hid_ready, hm_ready, hr_ready, y_ready, yT_ready, z_ready, z_read = (
            sem("e_mp_ready"), sem("e_mask_ready"), sem("e_hid_ready"), sem("e_hm_ready"), sem("e_hr_ready"),
            sem("e_y_ready"), sem("e_yT_ready"), sem("e_z_ready"), sem("e_z_read"))
        pv2_done, dve_step, pool_step, stored = sem("e_second_done"), sem("e_dve_step"), sem("e_pool_step"), sem("e_stored")
        block = ctx.enter_context(nc.Block())
        UN = 4 * E

        def walk(eng, step):
            step(0, 0, True, False)
            with eng.Fori(0, (NG - 2) // 2) as i:
                step(2 * i + 1, 1, False, False)
                step(2 * i + 2, 0, False, False)
            step(NG - 1, 1, False, True)

        @block.sync
        def _(sp):
            for dst, src in ((w1[:, :, :], a["L1_ffn_W1"].rearrange("e d h -> d e h")),
                             (w2[:, :, :, :].rearrange("p e c d -> p (e c) d"),
                              a["L1_ffn_W2"].rearrange("e (c p) d -> p (e c) d", p=P)),
                             (b2[:, :], a["L1_ffn_b2"]), (wg[:, :], a["L1_ffn_Wg"]),
                             (bg[:, :], a["L1_ffn_bg"].unsqueeze(0))):
                sp.dma_start(dst, src).then_inc(w_in, 16)
            for e in range(E):
                sp.dma_start(b1[:, e, :], a["L1_ffn_b1"].rearrange("e (c p) -> e p c", p=P)[e]).then_inc(w_in, 16)
            out = k.out.rearrange("b (h p) d -> p (b h) d", p=P)

            def step(g, par, first, last):
                sp.wait_ge(z_read, g + 1)
                sp.dma_start(out[:, bass.ds(g * GT, GT), :], group(X, g)).then_inc(stored, 16)
            walk(sp, step)
            sp.wait_ge(stored, 16 * NG)

        @block.gpsimd
        def _(pool):
            g_ = nc.gpsimd
            st = Steps(pool, pool_step)
            st.add(g_.iota(rank[:, :], [[-1, E]], base=E, channel_multiplier=0, allow_small_or_imprecise_dtypes=True))
            st.link(g_.memset(sel[:, :, :], 0.0))
            st.link(g_.affine_select(out=sel[:, :, :], in_=sel[:, :, :], compare_op=ALU.not_equal, fill=1.0, base=0,
                                     pattern=[[-1, E], [0, P]], channel_multiplier=1))
            pool.sem_inc(consts, 1)
            n_e.on_gpsimd(pool, k.mhalf, 0)

            def step(g, par, first, last):
                if not last:
                    n_e.on_gpsimd(pool, k.mhalf, g + 1)
            walk(pool, step)

        @block.vector
        def _(dve):
            v = nc.vector
            st = Steps(dve, dve_step)
            dve.wait_ge(consts, 1)

            def begin(g, par):
                n_e.on_vector(dve, st, group(X, g), hn[par], g)
                dve.sem_inc(hn_ready, 1)

            def choose(g):
                dve.wait_ge(lg_ready, g + 1)
                l = small[:, 0:GT * E].rearrange("p (j e) -> p j e", e=E)
                st.link(v.tensor_reduce(mx[:, :], l, AX.X, ALU.max))
                st.link(v.tensor_tensor(lg[:, :, :], l, over(mx[:, :], E), ALU.is_equal))
                st.link(v.tensor_tensor(lg[:, :, :], lg[:, :, :], rows(rank[:, :], GT), ALU.mult))
                st.link(v.tensor_reduce(mx[:, :], lg[:, :, :], AX.X, ALU.max))
                st.link(v.tensor_tensor(oh[:, :, :], lg[:, :, :], over(mx[:, :], E), ALU.is_equal))
                dve.sem_inc(oh_ready, 1)

            def finish(g):
                dve.wait_ge(z_ready, g + 1)
                x = group(X, g)
                st.link(v.scalar_tensor_tensor(out=x, in0=zp[:, :].rearrange("p (j d) -> p j d", j=GT),
                                               scalar=k.TG[:, 3:4], in1=x, op0=ALU.mult, op1=ALU.add))
                dve.sem_inc(z_read, 1)

            def step(g, par, first, last):
                for u in range(UN):
                    e, c = u // 4, u % 4
                    if c == 0:
                        dve.wait_ge(mask_ready, E * g + e + 1)
                    dve.wait_ge(hid_ready, UN * g + u + 1)
                    if not (first and u < 2):
                        dve.wait_ge(hr_ready, UN * g + u - 1)
                    v.scalar_tensor_tensor(out=hm[u % 2][:, :], in0=hp[u % 2][:, :],
                                           scalar=b1[:, e, c:c + 1], in1=mask[e % 2][:, :], op0=ALU.add,
                                           op1=ALU.mult).then_inc(hm_ready, 1)
                    if u == 2 and not first:
                        finish(g - 1)
                    if u == 8 and not last:
                        begin(g + 1, 1 - par)
                    if u == 20 and not last:
                        choose(g + 1)
                st.restart()

            dve.wait_ge(w_in, 16 * (5 + E))
            begin(0, 0)
            choose(0)
            walk(dve, step)
            finish(NG - 1)

        @block.tensor
        def _(pe):
            t = nc.tensor
            pe.wait_ge(w_in, 16 * (5 + E))
            pe.wait_ge(consts, 1)

            def begin(g, par):
                pe.wait_ge(hn_ready, g + 1)
                for j in range(GT):
                    ins = t.transpose(tp[:, j * P:j * P + P], hn[par][:, j, :], ident[:, :])
                ins.then_inc(tp_ready, 1)

            def score(g, par):
                pe.wait_ge(hT_ready, g + 1)
                for j in range(GT):
                    t.matmul(small[:, j * E:j * E + E], hT[par][:, j * P:j * P + P], wg[:, :], start=True, stop=False)
                    ins = t.matmul(small[:, j * E:j * E + E], k.ones[0:1, :], bg[:, :], start=False, stop=True)
                ins.then_inc(lg_ready, 1)

            def choice(g):
                pe.wait_ge(oh_ready, g + 1)
                for j in range(GT):
                    ins = t.transpose(tp[0:E, j * P:j * P + P], oh[:, j, :], ident[:, :])
                ins.then_inc(ohp_ready, 1)

            def mask_of(g, e, par, started):
                if e == 0:
                    pe.wait_ge(ohT_ready, 2 * g + 2)
                if started:
                    pe.wait_ge(mask_ready, E * g + e)
                t.matmul(mp[:, :], sel[:, e, :], ohTb[par][:, :], start=True, stop=True).then_inc(mp_ready, 1)

            def second(g, par, u):
                e, c = u // 4, u % 4
                pe.wait_ge(hr_ready, UN * g + u + 1)
                t.matmul(yp[:, :], w2[:, e, c, :], hr[u % 2][:, :], start=(u == 0), stop=False).then_inc(pv2_done, 1)

            def step(g, par, first, last):
                for u in range(UN):
                    e, c = u // 4, u % 4
                    if u == 0 and first:
                        mask_of(g, 0, par, False)
                    if c == 1 and e < E - 1:
                        mask_of(g, e + 1, par, True)
                    if not (first and u < 2):
                        pe.wait_ge(hm_ready, UN * g + u - 1)
                    t.matmul(hp[u % 2][:, :], w1[:, e, c * P:c * P + P], hT[par][:, :], start=True, stop=True
                             ).then_inc(hid_ready, 1)
                    if u == 0 and not first:
                        second(g - 1, 1 - par, UN - 1)
                        t.matmul(yp[:, :], b2[:, :], ohT[1 - par][:, :], start=False, stop=True).then_inc(y_ready, 1)
                    if u == 1 and not first:
                        pe.wait_ge(yT_ready, g)
                    if u == 2 and not first:
                        back(g - 1)
                    if u >= 1:
                        second(g, par, u - 1)
                    if u == 12 and not last:
                        begin(g + 1, 1 - par)
                    if u == 16 and not last:
                        score(g + 1, 1 - par)
                    if u == 24 and not last:
                        choice(g + 1)
                    if u == UN - 1 and not last:
                        mask_of(g + 1, 0, 1 - par, True)

            def back(g):
                for j in range(GT):
                    ins = t.transpose(zp[:, j * P:j * P + P], yT[:, j * P:j * P + P], ident[:, :])
                ins.then_inc(z_ready, 1)

            begin(0, 0)
            score(0, 0)
            choice(0)
            walk(pe, step)
            second(NG - 1, 1, UN - 1)
            t.matmul(yp[:, :], b2[:, :], ohT[1][:, :], start=False, stop=True).then_inc(y_ready, 1)
            pe.wait_ge(yT_ready, NG)
            back(NG - 1)

        @block.scalar
        def _(act):
            s_ = nc.scalar

            def begin(g, par):
                act.wait_ge(tp_ready, g + 1)
                s_.copy(hT[par][:, :], tp[:, :]).then_inc(hT_ready, 1)

            def choice(g, par):
                act.wait_ge(ohp_ready, g + 1)
                s_.copy(ohT[par][:, :], tp[0:E, :]).then_inc(ohT_ready, 1)
                s_.copy(ohTb[par][:, :], tp[0:E, :]).then_inc(ohT_ready, 1)

            def mask_of(g, e, started):
                act.wait_ge(mp_ready, E * g + e + 1)
                if started:
                    act.wait_ge(hm_ready, UN * g + 4 * (e - 1))
                s_.copy(mask[e % 2][:, :], mp[:, :]).then_inc(mask_ready, 1)

            def back(g):
                act.wait_ge(y_ready, g + 1)
                s_.copy(yT[:, :], yp[:, :]).then_inc(yT_ready, 1)

            def step(g, par, first, last):
                for u in range(UN):
                    e, c = u // 4, u % 4
                    if u == 0 and first:
                        mask_of(g, 0, False)
                    if c == 1 and e < E - 1:
                        mask_of(g, e + 1, not (first and e < 1))
                    act.wait_ge(hm_ready, UN * g + u + 1)
                    if not (first and u < 2):
                        act.wait_ge(pv2_done, UN * g + u - 1)
                    s_.activation(hr[u % 2][:, :], hm[u % 2][:, :], ACT.Relu).then_inc(hr_ready, 1)
                    if u == 0 and not first:
                        back(g - 1)
                    if u == 12 and not last:
                        begin(g + 1, 1 - par)
                    if u == 24 and not last:
                        choice(g + 1, 1 - par)
                    if u == UN - 1 and not last:
                        mask_of(g + 1, 0, True)

            begin(0, 0)
            choice(0, 0)
            walk(act, step)
            back(NG - 1)


class Kept:
    pass


def flamingo_kernel(nc, a, out):
    with ExitStack() as ctx:
        k = Kept()
        ctx.enter_context(nc.allow_non_contiguous_dma(reason="hidden biases, a few KB, laid out by channel"))

        def sb(name, shape, dt=F32):
            return ctx.enter_context(nc.sbuf_tensor(name, shape, dt))

        def dram(name, shape, dt=F32):
            return nc.dram_tensor(name, shape, dt, kind="Internal").ap()

        k.out = out
        k.X = sb("X", [P, T, D])
        k.ident = sb("ident", [P, P])
        k.ones = sb("ones", [1, P])
        k.mhalf = sb("mhalf", [P, T])
        k.TG = sb("TG", [P, 4])
        k.wq1, k.wo1 = sb("wq1", [P, D]), sb("wo1", [P, D])
        k.bq1, k.bo1 = sb("bq1", [P, 1]), sb("bo1", [1, D])
        k.maskrow = dram("maskrow", [B, NK])
        k.film_out = dram("film_out", [T, P, 2 * D])
        k.kern, k.kernpad = dram("kern", [P, L]), dram("kernpad", [P, 3 * P])
        k.keys = dram("keys", [B, 3, P, NK], BF16)
        k.values = dram("values", [B, P, KT * D])
        k.queries = dram("queries", [3, P, B * S], BF16)
        k.guards = dram("guards", [2, 3 * H1, S], BF16)

        with ExitStack() as layer0:
            def sb0(name, shape, dt=F32):
                return layer0.enter_context(nc.sbuf_tensor(name, shape, dt))

            k.w1_0, k.w2_0 = sb0("w1_0", [P, HID]), sb0("w2_0", [P, 4, D])
            k.b1_0, k.b2_0 = sb0("b1_0", [P, 4]), sb0("b2_0", [1, D])
            k.wg0, k.wm0, k.bm0 = sb0("wg0", [P, E]), sb0("wm0", [P, E, D]), sb0("bm0", [E, D])

            def later_loads(a):
                return ((k.wq1[:, :], a["L1_xattn_w_q"]), (k.wo1[:, :], a["L1_xattn_w_o"]),
                        (k.bq1[:, :], a["L1_xattn_b_q"].unsqueeze(1)), (k.bo1[:, :], a["L1_xattn_b_o"].unsqueeze(0)),
                        (k.wk1[:, :], a["L1_xattn_w_k"]), (k.wv1[0:C, :], a["L1_xattn_w_v"]),
                        (k.bk1[:, :], a["L1_xattn_b_k"].unsqueeze(1)),
                        (k.w1_0[:, :], a["L0_xattn_W1"]), (k.w2_0[:, :, :], a["L0_xattn_W2"].rearrange("(c p) d -> p c d", p=P)),
                        (k.b1_0[:, :], a["L0_xattn_b1"].rearrange("(c p) -> p c", p=P)),
                        (k.b2_0[:, :], a["L0_xattn_b2"].unsqueeze(0)),
                        (k.wg0[:, :], a["L0_ffn_wg"]), (k.bm0[:, :], a["L0_ffn_b"]))

            k.later_loads = later_loads
            with ExitStack() as attn0:
                def sba(name, shape, dt=F32):
                    return attn0.enter_context(nc.sbuf_tensor(name, shape, dt))

                k.X0 = sba("X0", [P, T, D])
                k.XF = sba("XF", [P, T, D])
                with ExitStack() as folded:
                    def sbf(name, shape, dt=F32):
                        return folded.enter_context(nc.sbuf_tensor(name, shape, dt))

                    k.WVF = sbf("WVF", [C + 1, 4 * D])
                    k.G = sbf("G", [P, H0 * C])
                    k.wk1, k.wv1, k.bk1 = sbf("wk1", [C, D]), sbf("wv1", [C + 2, D]), sbf("bk1", [P, 1])
                    k.tmask = sbf("tmask", [P, T])
                    setup_phase(nc, a, k)
                    attention0_phase(nc, a, k)
                k.Y = sba("Y", [P, T, D])
                k.FO = sba("FO", [P, T, 2 * D])
                conv_phase(nc, a, k)
                ffn0_phase(nc, a, k)
            mixture0_phase(nc, a, k)
        queries_phase(nc, a, k)
        attention1_phase(nc, a, k)
        mixture1_phase(nc, a, k)


_OUT = ((B, S, D), "float32")


def kernel(**inputs):
    import numpy as _np
    import concourse.bacc as _bacc
    from concourse import mybir as _mybir
    from concourse.bass_utils import run_bass_kernel_spmd as _run

    nc = _bacc.Bacc("TRN2", target_bir_lowering=False, num_devices=1)
    arrays, args = {}, {}
    for name, value in inputs.items():
        x = _np.ascontiguousarray(value)
        if x.dtype == _np.bool_:
            x = x.view(_np.uint8)
        x = x.reshape(x.shape or (1,))
        arrays[f"in_{name}_dram"] = x
        args[name] = nc.dram_tensor(f"in_{name}_dram", x.shape, _mybir.dt.from_np(x.dtype), kind="ExternalInput").ap()
    out = nc.dram_tensor("out_dram", _OUT[0], _mybir.dt.from_np(_np.dtype(_OUT[1])), kind="ExternalOutput").ap()
    flamingo_kernel(nc, args, out)
    r = _run(nc, [arrays], core_ids=[0])
    return r.results[0]["out_dram"]
```
